# Optimizing a Trainium2 kernel written in Bass

```python
import numpy as np
import jax
import jax.numpy as jnp

def _softmax(x, axis=-1):
    return jax.nn.softmax(x, axis=axis)

def _gelu(x):
    return jax.nn.gelu(x, approximate=True)

def _silu(x):
    return jax.nn.silu(x)

def _sigmoid(x):
    return jax.nn.sigmoid(x)

def _layernorm(x, axis=-1, eps=1e-05):
    m = jnp.mean(x, axis=axis, keepdims=True)
    v = jnp.var(x, axis=axis, keepdims=True)
    return (x - m) / jnp.sqrt(v + eps)

def _scatter_add(tgt, idx, src, axis=0):
    return tgt.at[idx].add(src)

def _segment_sum(src, seg, n):
    return jax.ops.segment_sum(src, seg, n)
kernel_name = 'mk_adj_preln_d2_adj_r2_e9e8a5'

def setup_inputs(seed: int=0):
    np.random.seed(seed)
    _w = jnp.asarray

    def _rec_inputs():
        import jax
        import jax.numpy as jnp
        _gk = jax.random.key(seed)
        x = 7.34e-05 + 1 * jax.random.normal(jax.random.fold_in(_gk, 1), (64, 128, 256), jnp.float32)
        _a = jax.random.bernoulli(jax.random.fold_in(_gk, 2), 0.0625, (128, 128))
        _a = jnp.logical_or(_a, jnp.swapaxes(_a, -1, -2))
        _a = jnp.logical_or(_a, jnp.eye(128, dtype=bool))
        _af = _a.astype(jnp.float32)
        adj = _af
        return (x, adj)
    x, adj = _rec_inputs()

    def _L0_gnn_setup():
        import jax, jax.numpy as jnp
        import numpy as np
        B, N, D, H = (16, 1025, 256, 8)
        LN_EPS = 1e-05

        def _make_mask(key, n):
            n_proto = n - 1
            adj = jax.random.bernoulli(key, 0.03, (n_proto, n_proto)).astype(jnp.float32)
            adj = jnp.clip(adj + adj.T + jnp.eye(n_proto, dtype=jnp.float32), 0.0, 1.0)
            mask = jnp.zeros((n, n), dtype=jnp.float32)
            mask = mask.at[0, :].set(1.0).at[:, 0].set(1.0)
            mask = mask.at[1:, 1:].set(adj)
            return mask
        key = jax.random.key(seed)
        ks = jax.random.split(key, 7)
        s = 1.0 / np.sqrt(D)
        return {'x': jax.random.normal(ks[0], (B, N, D), dtype=jnp.float32), 'w_qkv': jax.random.uniform(ks[1], (D, 3 * D), dtype=jnp.float32, minval=-s, maxval=s), 'w_proj': jax.random.uniform(ks[2], (D, D), dtype=jnp.float32, minval=-s, maxval=s), 'b_proj': jnp.zeros((D,), dtype=jnp.float32), 'ln_gamma': jnp.ones((D,), dtype=jnp.float32), 'ln_beta': jnp.zeros((D,), dtype=jnp.float32), 'attn_mask': _make_mask(ks[3], N)}
    _L0_gnn_all = _L0_gnn_setup()
    _L0_gnn_in = {k: v for k, v in _L0_gnn_all.items() if k in ('w_qkv', 'w_proj', 'b_proj', 'ln_gamma', 'ln_beta')}
    del _L0_gnn_all

    def _L1_gnn_setup():
        import jax, jax.numpy as jnp
        import numpy as np
        B, N, D, H = (4, 1024, 256, 8)
        HD = D // H
        key = jax.random.key(seed)
        ks = jax.random.split(key, 10)
        x = jax.random.normal(ks[0], (B, N, D), dtype=jnp.float32)
        adj = (jax.random.uniform(ks[1], (N, N)) < 0.1).astype(jnp.float32)
        s = 1.0 / np.sqrt(D)
        Wq = jax.random.normal(ks[2], (D, D), dtype=jnp.float32) * s
        Wk = jax.random.normal(ks[3], (D, D), dtype=jnp.float32) * s
        Wv = jax.random.normal(ks[4], (D, D), dtype=jnp.float32) * s
        Wo = jax.random.normal(ks[5], (D, D), dtype=jnp.float32) * s
        bq = jnp.zeros((D,), jnp.float32)
        bk = jnp.zeros((D,), jnp.float32)
        bv = jnp.zeros((D,), jnp.float32)
        bo = jnp.zeros((D,), jnp.float32)
        return {'x': x, 'adj': adj, 'Wq': Wq, 'bq': bq, 'Wk': Wk, 'bk': bk, 'Wv': Wv, 'bv': bv, 'Wo': Wo, 'bo': bo}
    _L1_gnn_all = _L1_gnn_setup()
    _L1_gnn_in = {k: v for k, v in _L1_gnn_all.items() if k in ('Wq', 'bq', 'Wk', 'bk', 'Wv', 'bv', 'Wo', 'bo')}
    del _L1_gnn_all
    return {'x': x, 'adj': adj, 'L0_gnn_w_qkv': _L0_gnn_in['w_qkv'], 'L0_gnn_w_proj': _L0_gnn_in['w_proj'], 'L0_gnn_b_proj': _L0_gnn_in['b_proj'], 'L0_gnn_ln_gamma': _L0_gnn_in['ln_gamma'], 'L0_gnn_ln_beta': _L0_gnn_in['ln_beta'], 'L1_gnn_Wq': _L1_gnn_in['Wq'], 'L1_gnn_bq': _L1_gnn_in['bq'], 'L1_gnn_Wk': _L1_gnn_in['Wk'], 'L1_gnn_bk': _L1_gnn_in['bk'], 'L1_gnn_Wv': _L1_gnn_in['Wv'], 'L1_gnn_bv': _L1_gnn_in['bv'], 'L1_gnn_Wo': _L1_gnn_in['Wo'], 'L1_gnn_bo': _L1_gnn_in['bo']}

def reference(x, adj, L0_gnn_w_qkv, L0_gnn_w_proj, L0_gnn_b_proj, L0_gnn_ln_gamma, L0_gnn_ln_beta, L1_gnn_Wq, L1_gnn_bq, L1_gnn_Wk, L1_gnn_bk, L1_gnn_Wv, L1_gnn_bv, L1_gnn_Wo, L1_gnn_bo):
    import jax
    import jax.numpy as jnp

    def _L0_gnn_ref(x, w_qkv, w_proj, b_proj, ln_gamma, ln_beta, attn_mask):
        import jax, jax.numpy as jnp
        import numpy as np
        B, N, D, H = (16, 1025, 256, 8)
        LN_EPS = 1e-05

        def _make_mask(key, n):
            n_proto = n - 1
            adj = jax.random.bernoulli(key, 0.03, (n_proto, n_proto)).astype(jnp.float32)
            adj = jnp.clip(adj + adj.T + jnp.eye(n_proto, dtype=jnp.float32), 0.0, 1.0)
            mask = jnp.zeros((n, n), dtype=jnp.float32)
            mask = mask.at[0, :].set(1.0).at[:, 0].set(1.0)
            mask = mask.at[1:, 1:].set(adj)
            return mask
        b, n, d = x.shape
        hd = d // H
        scale = hd ** (-0.5)
        qkv = (x @ w_qkv).reshape(b, n, 3, H, hd).transpose(2, 0, 3, 1, 4)
        q, k, v = (qkv[0], qkv[1], qkv[2])
        attn = jnp.einsum('bhnd,bhmd->bhnm', q, k) * scale
        attn = jnp.where(attn_mask[None, None] == 0, -jnp.inf, attn)
        attn = jax.nn.softmax(attn, axis=-1)
        o = jnp.einsum('bhnm,bhmd->bhnd', attn, v).transpose(0, 2, 1, 3).reshape(b, n, d)
        o = o @ w_proj + b_proj
        mu = jnp.mean(o, axis=-1, keepdims=True)
        var = jnp.mean(jnp.square(o - mu), axis=-1, keepdims=True)
        ln = (o - mu) * jax.lax.rsqrt(var + LN_EPS) * ln_gamma + ln_beta
        return o + ln

    def _L1_gnn_ref(x, adj, Wq, bq, Wk, bk, Wv, bv, Wo, bo):
        import jax, jax.numpy as jnp
        import numpy as np
        B, N, D, H = (4, 1024, 256, 8)
        HD = D // H
        b, n, d = x.shape
        q = (x @ Wq + bq).reshape(b, n, H, HD)
        k = (x @ Wk + bk).reshape(b, n, H, HD)
        v = (x @ Wv + bv).reshape(b, n, H, HD)
        scores = jnp.einsum('bqhd,bkhd->bhqk', q, k) / jnp.sqrt(jnp.float32(HD))
        scores = scores + (1.0 - adj)[None, None, :, :] * -1000000000.0
        attn = jax.nn.softmax(scores, axis=-1)
        out = jnp.einsum('bhqk,bkhd->bqhd', attn, v).reshape(b, n, d)
        return out @ Wo + bo
    h = jnp.maximum(_layernorm(x, axis=-1), 0.0)
    x = x + _L0_gnn_ref(h, L0_gnn_w_qkv, L0_gnn_w_proj, L0_gnn_b_proj, L0_gnn_ln_gamma, L0_gnn_ln_beta, adj)
    h = jnp.maximum(_layernorm(x, axis=-1), 0.0)
    x = x + _L1_gnn_ref(h, adj, L1_gnn_Wq, L1_gnn_bq, L1_gnn_Wk, L1_gnn_bk, L1_gnn_Wv, L1_gnn_bv, L1_gnn_Wo, L1_gnn_bo)
    return x

_drawn_inputs = setup_inputs


def setup_inputs(seed=0):
    import zlib

    import numpy as np

    out = dict(_drawn_inputs(seed))
    spreads = {'L0_gnn_b_proj': (0.0, 0.1),
     'L0_gnn_ln_gamma': (1.0, 0.2),
     'L0_gnn_ln_beta': (0.0, 0.1),
     'L1_gnn_bq': (0.0, 0.8),
     'L1_gnn_bk': (0.0, 0.8),
     'L1_gnn_bv': (0.0, 0.1),
     'L1_gnn_bo': (0.0, 0.1)}
    factors = {'L1_gnn_Wq': 3.035, 'L1_gnn_Wk': 2.884}
    for name, (base, spread) in spreads.items():
        noise = np.random.default_rng([zlib.crc32(name.encode()), seed]).standard_normal(out[name].shape)
        drawn = base * np.exp(spread * noise) if base else spread * noise
        out[name] = jnp.asarray(drawn.astype(out[name].dtype))
    for name, factor in factors.items():
        out[name] = (out[name] * factor).astype(out[name].dtype)
    return out
```

```python
import concourse.bass as bass
from concourse import mybir
from contextlib import ExitStack

fp32 = mybir.dt.float32
ALU = mybir.AluOpType
ACT = mybir.ActivationFunctionType

BATCHES, TOK, D, HEADS = 64, 128, 256, 8
HD = D // HEADS
KC = D // 128
QUADS = 128 // HD
G = 4
GROUPS = BATCHES // G
UNITS = 2 * BATCHES
SLOTS = 8
LN_EPS = 1e-5
SCALE = float(HD) ** -0.5
MASKED_FIRST = 1e30
MASKED_SECOND = 1e9

UNIT_OF_SLOT = [("A", 0), ("A", 1), ("A", 2), ("B", 0), ("A", 3), ("B", 1), ("B", 2), ("B", 3)]
PIECES = [
    ([("QK", "B", 0)], [("V", "B", 0)]),
    ([("QK", "B", 1)], [("V", "B", 1)]),
    ([("QK", "B", 2)], [("QK", "B", 3)]),
    ([("V", "B", 2), ("T", "A", 0), ("T", "A", 1), ("T", "A", 2), ("T", "A", 3)], [("V", "B", 3)]),
    ([("QK", "A", 0)], [("V", "A", 0)]),
    ([("QK", "A", 1)], [("V", "A", 1)]),
    ([("QK", "A", 2)], [("V", "A", 2), ("T", "B", 0), ("T", "B", 1), ("T", "B", 2)]),
    ([("QK", "A", 3)], [("V", "A", 3), ("T", "B", 3)]),
]
NORM_ATTN_SLOTS = (2, 3, 4, 6)
X_BETA_SLOTS = (3, 4, 5, 7)
FIRST_PIECES = [("T", "A", b) for b in range(G)] + [(k, "A", i) for i in range(G) for k in ("QK", "V")]


def wait_apart(engine, semaphore, value, passed):
    engine.wait_ge(semaphore, value)
    engine.sem_inc(passed, 1)


class Pass:

    def __init__(self, g, a=True, b=True, ahead=True):
        self.g, self.a, self.b, self.ahead = g, a, b, ahead
        self.first, self.last = not b, not a

    def active(self, slot):
        return self.a if UNIT_OF_SLOT[slot][0] == "A" else self.b

    def unit(self, slot):
        before = sum(self.active(s) for s in range(slot))
        if self.first:
            return before
        if self.last:
            return UNITS - G + before
        return self.g * SLOTS - G + before

    def pieces(self, slot, half):
        out = []
        for kind, stream, i in PIECES[slot][half]:
            if stream == "A" and self.ahead:
                out.append((kind, stream, i, self.g + 1))
            if stream == "B" and kind == "T" and self.a:
                out.append((kind, stream, i, self.g))
            if stream == "B" and kind != "T" and self.b:
                out.append((kind, stream, i, self.g - 1))
        return out

    def finished(self, slot):
        if slot > 0:
            if not self.active(slot - 1):
                return None
            stream, b = UNIT_OF_SLOT[slot - 1]
            return stream, b, (self.g if stream == "A" else self.g - 1), self.unit(slot - 1)
        if isinstance(self.g, int) and self.g < 2:
            return None
        return "B", G - 1, self.g - 2, self.unit(0) - 1


HEAD_ORDER = [q + QUADS * c for q in range(QUADS) for c in range(KC)]
END = ("B", G - 1, GROUPS - 1, UNITS - 1)


def each_slot(engine, slot_of):
    for slot in range(SLOTS):
        slot_of(Pass(0, b=False), slot)
    slot_of(Pass(1), 0)
    with engine.Fori(1, GROUPS - 1) as g:
        for slot in range(1, SLOTS):
            slot_of(Pass(g), slot)
        slot_of(Pass(g + 1), 0)
    for slot in range(1, SLOTS):
        slot_of(Pass(GROUPS - 1, ahead=False), slot)
    for slot in range(SLOTS):
        slot_of(Pass(GROUPS, a=False, ahead=False), slot)


def unit_of_b(b, group):
    return (group + 1) * SLOTS - G + UNIT_OF_SLOT.index(("B", b))


def gnn_stack_kernel(nc, x, adj, w_qkv, w_proj, b_proj, ln_gamma, ln_beta,
                     Wq, bq, Wk, bk, Wv, bv, Wo, bo, out):
    ctx = ExitStack()
    with ctx:
        def sb(name, shape, dt=fp32):
            return ctx.enter_context(nc.sbuf_tensor(name, shape, dt))

        def bank(name):
            return ctx.enter_context(nc.psum_tensor(name, [128, 512], fp32))

        def sem(name):
            return ctx.enter_context(nc.semaphore(name))

        def per_stream(name):
            return {"A": sem(name + "_a"), "B": sem(name + "_b")}

        w_in = {s: sb(f"w_in_{s}", [128, KC, 3 * D]) for s in "AB"}
        w_out = {s: sb(f"w_out_{s}", [128, KC, D]) for s in "AB"}
        adjacency = sb("adjacency", [TOK, TOK])
        penalty = {s: sb(f"penalty_{s}", [TOK, TOK]) for s in "AB"}
        ident = sb("ident", [128, 128])
        gamma_row = sb("gamma_row", [128, D])
        beta_row = sb("beta_row", [128, D])
        bproj_row = sb("bproj_row", [128, D])
        bo_row = sb("bo_row", [128, D])
        bqk_col = sb("bqk_col", [128, 2 * KC])
        bv_col = sb("bv_col", [128, KC])
        bv_wide = sb("bv_wide", [128, KC, 128])
        eps_col = sb("eps_col", [128, G])
        power_col = sb("power_col", [128, G])
        x_in = sb("x_in", [TOK, G, D])
        x_beta = sb("x_beta", [TOK, G, D])
        normed = {s: sb(f"normed_{s}", [TOK, G, D]) for s in "AB"}
        hT = {s: sb(f"hT_{s}", [128, KC, G * TOK]) for s in "AB"}
        qkT = {s: sb(f"qkT_{s}", [128, 2 * KC, G * TOK]) for s in "AB"}
        v = {s: sb(f"v_{s}", [TOK, G, D]) for s in "AB"}
        attn_out = sb("attn_out", [TOK, G, D])
        attn_ln = sb("attn_ln", [TOK, G, D])
        x_mid = sb("x_mid", [TOK, G, D])
        x_mid_bias = sb("x_mid_bias", [TOK, G, D])
        y = sb("y", [TOK, G, D])
        moments = {s: sb(f"moments_{s}", [TOK, G, 6]) for s in "ABO"}
        mean_var = {s: sb(f"mean_var_{s}", [TOK, G, 2]) for s in "ABO"}
        var_eps = {s: sb(f"var_eps_{s}", [TOK, G]) for s in "ABO"}
        rstd = {s: sb(f"rstd_{s}", [TOK, G]) for s in "ABO"}
        neg_scores = sb("neg_scores", [TOK, HEADS, TOK])
        neg_max = sb("neg_max", [TOK, HEADS])
        probs = sb("probs", [TOK, HEADS, TOK])
        row_sum = sb("row_sum", [TOK, HEADS])
        recip = sb("recip", [TOK, HEADS, HD])
        probsT = sb("probsT", [TOK, HEADS, TOK])
        recipT = sb("recipT", [128, KC, TOK])
        oT = sb("oT", [128, KC, TOK])

        head_bank = [bank(f"head_bank{j}") for j in range(QUADS)]
        half_bank = [bank(f"half_bank{j}") for j in range(2)]
        recip_out_bank = bank("recip_out_bank")
        oT_bank = bank("oT_bank")
        scores_ps = [head_bank[h % QUADS][:, (h // QUADS) * TOK:(h // QUADS + 1) * TOK] for h in range(HEADS)]
        rT_ps, out_ps, oT_ps = recip_out_bank[:, 0:256], recip_out_bank[:, 256:512], oT_bank[:, 0:256]

        s_weights, s_rows, s_adj = sem("weights_loaded"), sem("rows_loaded"), sem("adj_loaded")
        s_load = [sem(f"x_loaded{b}") for b in range(G)]
        s_store = [sem(f"y_stored{b}") for b in range(G)]
        s_pool_const, s_dve_const, s_bias_mm = sem("pool_consts"), sem("dve_consts"), sem("bias_product")
        s_scores, s_pT, s_rT = sem("scores_done"), sem("probsT_halves_done"), sem("recipT_done")
        s_pv, s_out = sem("pv_done"), sem("out_done")
        s_T, s_V, s_QK = per_stream("hT_done"), per_stream("v_done"), per_stream("qk_done")
        s_T_sb, s_V_sb, s_QK_sb = per_stream("hT_copied"), per_stream("v_copied"), per_stream("qk_copied")
        s_pT_sb = [sem("probsT_low_copied"), sem("probsT_high_copied")]
        s_rT_sb, s_oT_sb, s_out_read = sem("recipT_copied"), sem("oT_scaled"), sem("out_read")
        s_passed_dve, s_passed_sp = sem("dve_waits_passed"), sem("sp_waits_passed")
        s_negmax, s_exp, s_recip = sem("masked_with_max"), sem("exp_done"), sem("recip_done")
        s_moments = {s: sem(f"moments_done_{s}") for s in "ABO"}
        s_stats = {s: sem(f"stats_done_{s}") for s in "ABO"}
        s_vareps = {s: sem(f"vareps_done_{s}") for s in "ABO"}
        s_rstd = {s: sem(f"rstd_done_{s}") for s in "ABO"}
        s_norm = {s: sem(f"normed_{s}") for s in "ABO"}
        s_mid_part = sem("x_mid_parts")
        s_mid, s_mid_bias = sem("x_mid_done"), sem("x_mid_bias_done")
        s_xbeta = sem("x_beta_done")

        block = ctx.enter_context(nc.Block())

        DVE_CONSTS = 10

        @block.sync
        def _(sp):
            def load_x(b, group):
                sp.dma_start(x_in[:, b, :], x[group * G + b, :, :]).then_inc(s_load[b], 16)

            for b in range(G):
                load_x(b, 0)
            sp.dma_start(w_in["A"][:], w_qkv.rearrange("(c p) n -> p c n", p=128)).then_inc(s_weights, 16)
            sp.dma_start(w_out["A"][:], w_proj.rearrange("(c p) n -> p c n", p=128)).then_inc(s_weights, 16)
            sp.dma_start(adjacency[:], adj).then_inc(s_adj, 16)
            for i, w in enumerate((Wq, Wk, Wv)):
                sp.dma_start(w_in["B"][:, :, i * D:(i + 1) * D],
                             w.rearrange("(c p) n -> p c n", p=128)).then_inc(s_weights, 16)
            sp.dma_start(w_out["B"][:], Wo.rearrange("(c p) n -> p c n", p=128)).then_inc(s_weights, 16)
            for t, row in ((gamma_row, ln_gamma), (beta_row, ln_beta), (bproj_row, b_proj), (bo_row, bo)):
                sp.dma_start(t[:], row.rearrange("(a n) -> a n", a=1).broadcast_to([128, D])).then_inc(s_rows, 16)
            with nc.allow_non_contiguous_dma(reason="bias columns, 256 floats each"):
                for t, col in ((bqk_col[:, 0:KC], bq), (bqk_col[:, KC:2 * KC], bk), (bv_col[:], bv)):
                    sp.dma_start(t, col.rearrange("(c p) -> p c", p=128)).then_inc(s_rows, 16)

            def store(unit):
                if unit is not None and unit[0] == "B":
                    _, b, group, n = unit
                    wait_apart(sp, s_out_read, n + 1, s_passed_sp)
                    sp.dma_start(out[group * G + b, :, :], y[:, b, :]).then_inc(s_store[b], 16)

            def slot_of(p, slot):
                if p.ahead and slot == 1:
                    for b in range(G):
                        wait_apart(sp, s_norm["A"], (p.g + 1) * G, s_passed_sp)
                        wait_apart(sp, s_xbeta, p.g * G + b + 1, s_passed_sp)
                        load_x(b, p.g + 1)
                store(p.finished(slot))

            each_slot(sp, slot_of)
            store(END)
            for b in range(G):
                sp.wait_ge(s_store[b], 16 * GROUPS)

        @block.gpsimd
        def _(pool):
            nc.gpsimd.memset(ident[:], 0.0).then_inc(s_pool_const, 1)
            nc.gpsimd.memset(eps_col[:], LN_EPS).then_inc(s_pool_const, 1)
            nc.gpsimd.memset(power_col[:], -0.5).then_inc(s_pool_const, 1)
            pool.wait_ge(s_pool_const, 3)
            nc.gpsimd.affine_select(out=ident[:], in_=ident[:], compare_op=ALU.not_equal, fill=1.0, base=0,
                                    pattern=[[-1, 128]], channel_multiplier=1).then_inc(s_pool_const, 1)

            def rstd_of(kind, b0, n, group):
                count = group * (G // n) + b0 // n + 1
                pool.wait_ge(s_stats[kind], group * G + b0 + n)
                nc.gpsimd.tensor_tensor(var_eps[kind][:, b0:b0 + n], mean_var[kind][:, b0:b0 + n, 1],
                                        eps_col[:, 0:n], ALU.add).then_inc(s_vareps[kind], 1)
                pool.wait_ge(s_vareps[kind], count)
                nc.gpsimd.tensor_tensor(rstd[kind][:, b0:b0 + n], var_eps[kind][:, b0:b0 + n],
                                        power_col[:, 0:n], ALU.pow).then_inc(s_rstd[kind], 1)

            def x_beta_of(b, group):
                pool.wait_ge(s_load[b], (group + 1) * 16)
                if not (isinstance(group, int) and group == 0):
                    pool.wait_ge(s_mid, (group - 1) * G + b + 1)
                nc.gpsimd.tensor_tensor(x_beta[:, b, :], x_in[:, b, :], beta_row[:], ALU.add).then_inc(s_xbeta, 1)

            def x_mid_of(b, group):
                done = (group * G + b) * 2
                pool.wait_ge(s_norm["O"], group * G + b + 1)
                nc.gpsimd.tensor_tensor(attn_ln[:, b, :], attn_ln[:, b, :], gamma_row[:],
                                        ALU.mult).then_inc(s_mid_part, 1)
                pool.wait_ge(s_mid_part, done + 1)
                nc.gpsimd.tensor_tensor(attn_out[:, b, :], attn_out[:, b, :], attn_ln[:, b, :],
                                        ALU.add).then_inc(s_mid_part, 1)
                pool.wait_ge(s_mid_part, done + 2)
                pool.wait_ge(s_xbeta, group * G + b + 1)
                nc.gpsimd.tensor_tensor(x_mid[:, b, :], attn_out[:, b, :], x_beta[:, b, :],
                                        ALU.add).then_inc(s_mid, 1)

            def x_mid_bias_of(b, group):
                pool.wait_ge(s_mid, group * G + b + 1)
                if not (isinstance(group, int) and group == 0):
                    pool.wait_ge(s_out_read, unit_of_b(b, group - 1) + 1)
                nc.gpsimd.tensor_tensor(x_mid_bias[:, b, :], x_mid[:, b, :], bo_row[:],
                                        ALU.add).then_inc(s_mid_bias, 1)

            pool.wait_ge(s_rows, 16 * 7)
            for b in range(0, G, 2):
                rstd_of("A", b, 2, 0)
            for b in range(G):
                x_beta_of(b, 0)
            pool.wait_ge(s_dve_const, DVE_CONSTS)

            def slot_of(p, slot):
                if p.a and 4 <= slot:
                    rstd_of("B", slot - 4, 1, p.g)
                if p.ahead and slot in (2, 3):
                    rstd_of("A", 2 * (slot - 2), 2, p.g + 1)
                if p.a and slot in NORM_ATTN_SLOTS:
                    b = NORM_ATTN_SLOTS.index(slot)
                    rstd_of("O", b, 1, p.g)
                    x_mid_of(b, p.g)
                if p.ahead and slot in X_BETA_SLOTS:
                    x_beta_of(X_BETA_SLOTS.index(slot), p.g + 1)
                if slot == 0 and p.b:
                    x_mid_bias_of(2, p.g - 1)
                if slot == 1 and p.b:
                    x_mid_bias_of(3, p.g - 1)
                if slot == 5 and p.a:
                    x_mid_bias_of(0, p.g)
                if slot == 7 and p.a:
                    x_mid_bias_of(1, p.g)

            each_slot(pool, slot_of)

        @block.tensor
        def _(pe):
            copied = {"T": s_T_sb, "V": s_V_sb, "QK": s_QK_sb}

            def transposed_h(stream, b, group, units):
                pe.wait_ge(s_norm[stream], group * G + b + 1)
                if units is not None:
                    pe.wait_ge(s_negmax, units * HEADS)
                for c in range(KC):
                    mm = nc.tensor.transpose(head_bank[b][:, c * 128:(c + 1) * 128],
                                             normed[stream][:, b, c * 128:(c + 1) * 128], ident[:])
                mm.then_inc(s_T[stream], 1)

            def values(stream, b, group, bank):
                pe.wait_ge(s_T_sb[stream], group * G + b + 1)
                for c in range(KC):
                    mm = nc.tensor.matmul(bank[:, 0:D], hT[stream][:, c, b * TOK:(b + 1) * TOK],
                                          w_in[stream][:, c, 2 * D:3 * D], start=(c == 0), stop=(c == KC - 1))
                mm.then_inc(s_V[stream], 1)

            def queries_keys(stream, m, group, bank):
                pe.wait_ge(s_T_sb[stream], (group + 1) * G)
                for c in range(KC):
                    mm = nc.tensor.matmul(bank[:], w_in[stream][:, c, m * 128:(m + 1) * 128],
                                          hT[stream][:, c, :], start=(c == 0), stop=(c == KC - 1))
                mm.then_inc(s_QK[stream], 1)

            def piece_copied(p, slot, half):
                for kind, stream, i, group in p.pieces(slot, half):
                    if kind != "T":
                        pe.wait_ge(copied[kind][stream], group * G + i + 1)

            def piece_before_copied(p, slot, half):
                if slot > 0:
                    piece_copied(p, slot - 1, half)
                elif p.first or p.last:
                    piece_copied_at_ends(p, half)
                else:
                    pe.wait_ge((s_QK_sb, s_V_sb)[half]["A"], (p.g + 1) * G)

            def piece_copied_at_ends(p, half):
                if p.first:
                    pe.wait_ge((s_QK_sb, s_V_sb)[half]["A"], G)

            def pieces(p, slot, half, done):
                for kind, stream, i, group in p.pieces(slot, half):
                    if kind == "T":
                        transposed_h(stream, i, group, p.unit(slot) + p.active(slot))
                        continue
                    if done is not None:
                        pe.wait_ge(s_pT_sb[half], done[3] + 1)
                    piece_before_copied(p, slot, half)
                    (values if kind == "V" else queries_keys)(stream, i, group, half_bank[half])

            def scores(stream, b, group, n, p, slot):
                if b == 0:
                    pe.wait_ge(s_QK_sb[stream], (group + 1) * G)
                if not (p.first and slot == 0):
                    pe.wait_ge(s_negmax, n * HEADS)
                if slot > 0:
                    transposes = [q for half in range(2) for q in p.pieces(slot - 1, half) if q[0] == "T"]
                    for _, last_stream, last, its_group in transposes[-1:]:
                        pe.wait_ge(s_T_sb[last_stream], its_group * G + last + 1)
                elif not p.first:
                    pe.wait_ge(s_T_sb["B"], p.g * G)
                tokens = slice(b * TOK, (b + 1) * TOK)
                for h in range(HEADS):
                    c, lanes = h // QUADS, slice(HD * (h % QUADS), HD * (h % QUADS + 1))
                    nc.tensor.matmul(scores_ps[h], qkT[stream][lanes, c, tokens],
                                     qkT[stream][lanes, KC + c, tokens],
                                     start=True, stop=True).then_inc(s_scores, 1)

            def transposed_probs(n, p, slot):
                first = p is not None and p.first and slot == 1
                for half in range(2):
                    pe.wait_ge(s_exp, n * HEADS + 4 * (half + 1))
                    if not first:
                        pe.wait_ge(s_pT_sb[half], n)
                    if p is not None:
                        piece_before_copied(p, slot, half)
                    for i in range(4):
                        mm = nc.tensor.transpose(half_bank[half][:, i * TOK:(i + 1) * TOK],
                                                 probs[:, 4 * half + i, :], ident[:])
                    mm.then_inc(s_pT, 1)
                pe.wait_ge(s_recip, n + 1)
                if not first:
                    pe.wait_ge(s_out_read, n)
                for c in range(KC):
                    mm = nc.tensor.transpose(rT_ps[:, c * TOK:(c + 1) * TOK],
                                             recip[:, c * QUADS:(c + 1) * QUADS, :].rearrange("p h d -> p (h d)"),
                                             ident[:])
                mm.then_inc(s_rT, 1)

            def probs_values(stream, b, group, n):
                pe.wait_ge(s_V_sb[stream], group * G + b + 1)
                for half in range(2):
                    pe.wait_ge(s_pT_sb[half], n + 1)
                    if half == 0 and not (isinstance(n, int) and n == 0):
                        pe.wait_ge(s_oT_sb, n)
                    for i in range(4 * half, 4 * half + 4):
                        h = HEAD_ORDER[i]
                        c, lanes = h // QUADS, slice(HD * (h % QUADS), HD * (h % QUADS + 1))
                        mm = nc.tensor.matmul(oT_ps[lanes, c * TOK:(c + 1) * TOK],
                                              v[stream][:, b, h * HD:(h + 1) * HD],
                                              probsT[:, i, :], start=True, stop=True, skip_group_check=True)
                mm.then_inc(s_pv, 1)

            def output(stream, n):
                pe.wait_ge(s_oT_sb, n + 1)
                pe.wait_ge(s_rT_sb, n + 1)
                for c in range(KC):
                    mm = nc.tensor.matmul(out_ps, oT[:, c, :], w_out[stream][:, c, :],
                                          start=(c == 0), stop=(c == KC - 1))
                mm.then_inc(s_out, 1)

            def slot_of(p, slot):
                done = p.finished(slot)
                if done is not None:
                    transposed_probs(done[3], p, slot)
                if p.active(slot):
                    stream, b = UNIT_OF_SLOT[slot]
                    scores(stream, b, p.g if stream == "A" else p.g - 1, p.unit(slot), p, slot)
                if done is not None:
                    probs_values(*done)
                pieces(p, slot, 0, done)
                if done is not None:
                    output(done[0], done[3])
                pieces(p, slot, 1, done)

            pe.wait_ge(s_pool_const, 4)
            pe.wait_ge(s_dve_const, DVE_CONSTS - 1)
            for c in range(KC):
                mm = nc.tensor.matmul(out_ps, bv_wide[:, c, :], w_out["B"][:, c, :], start=(c == 0), stop=(c == KC - 1))
            mm.then_inc(s_bias_mm, 1)
            pe.wait_ge(s_dve_const, DVE_CONSTS)
            for kind, stream, i in FIRST_PIECES:
                if kind == "T":
                    transposed_h(stream, i, 0, None)
                    continue
                if i > 0:
                    pe.wait_ge(copied[kind][stream], i)
                if kind == "QK":
                    queries_keys(stream, i, 0, half_bank[0])
                else:
                    values(stream, i, 0, half_bank[1])
            each_slot(pe, slot_of)
            transposed_probs(END[3], None, None)
            probs_values(*END)
            output(END[0], END[3])

        @block.scalar
        def _(act):
            def copy_piece(kind, stream, i, group, half):
                if kind == "T":
                    act.wait_ge(s_T[stream], group * G + i + 1)
                    nc.scalar.activation(hT[stream][:, :, i * TOK:(i + 1) * TOK],
                                         head_bank[i][:, 0:256].rearrange("p (c t) -> p c t", c=KC),
                                         ACT.Relu).then_inc(s_T_sb[stream], 1)
                if kind == "V":
                    act.wait_ge(s_V[stream], group * G + i + 1)
                    nc.scalar.copy(v[stream][:, i, :], half_bank[half][:, 0:D]).then_inc(s_V_sb[stream], 1)

            def tail(done):
                n = done[3]
                act.wait_ge(s_pT, 2 * n + 1)
                nc.scalar.copy(probsT[:, 0:4, :].rearrange("p h t -> p (h t)"), half_bank[0][:]).then_inc(s_pT_sb[0], 1)
                act.wait_ge(s_rT, n + 1)
                nc.scalar.copy(recipT[:].rearrange("p c t -> p (c t)"), rT_ps).then_inc(s_rT_sb, 1)

            def exps(n):
                for i, h in enumerate(HEAD_ORDER):
                    act.wait_ge(s_negmax, n * HEADS + i + 1)
                    nc.scalar.activation(probs[:, i, :], neg_scores[:, i, :], ACT.Exp, scale=-1.0,
                                         bias=neg_max[:, h:h + 1], accum_out=row_sum[:, h:h + 1]).then_inc(s_exp, 1)

            def slot_of(p, slot):
                done = p.finished(slot)
                if done is not None:
                    tail(done)
                if p.active(slot):
                    exps(p.unit(slot))
                for half in range(2):
                    for q in p.pieces(slot, half):
                        copy_piece(*q, half)

            for q in FIRST_PIECES:
                copy_piece(*q, 0, 1)
            each_slot(act, slot_of)
            tail(END)

        @block.vector
        def _(dve):
            count = [0]

            def const(ins):
                count[0] += 1
                ins.then_inc(s_dve_const, 1)
                dve.wait_ge(s_dve_const, count[0])

            def stats(kind, source, b, group):
                nc.vector.bn_stats(moments[kind][:, b, :], source).then_inc(s_moments[kind], 1)
                wait_apart(dve, s_moments[kind], group * G + b + 1, s_passed_dve)
                nc.vector.bn_aggr(mean_var[kind][:, b, :], moments[kind][:, b, :]).then_inc(s_stats[kind], 1)

            def stats_in(b, group):
                dve.wait_ge(s_load[b], (group + 1) * 16)
                stats("A", x_in[:, b, :], b, group)

            def stats_mid(b, group):
                dve.wait_ge(s_mid, group * G + b + 1)
                stats("B", x_mid[:, b, :], b, group)

            def norm(kind, target, source, b, group):
                nc.vector.tensor_scalar(target[:, b, :], source[:, b, :], mean_var[kind][:, b, 0:1],
                                        rstd[kind][:, b:b + 1], ALU.subtract, ALU.mult).then_inc(s_norm[kind], 1)

            def norm_in(pair, group):
                dve.wait_ge(s_rstd["A"], group * 2 + pair + 1)
                for b in (2 * pair, 2 * pair + 1):
                    norm("A", normed["A"], x_in, b, group)

            def norm_mid(b, group):
                dve.wait_ge(s_rstd["B"], group * G + b + 1)
                norm("B", normed["B"], x_mid, b, group)

            def norm_attn(b, group):
                dve.wait_ge(s_rstd["O"], group * G + b + 1)
                norm("O", attn_ln, attn_out, b, group)

            def recip_of(n):
                dve.wait_ge(s_exp, (n + 1) * HEADS)
                nc.vector.reciprocal(recip[:], row_sum[:].unsqueeze(2).to_broadcast([TOK, HEADS, HD])).then_inc(s_recip, 1)

            def probsT_high(n):
                dve.wait_ge(s_pT, 2 * n + 2)
                nc.vector.tensor_copy(probsT[:, 4:8, :].rearrange("p h t -> p (h t)"),
                                      half_bank[1][:]).then_inc(s_pT_sb[1], 1)

            def mask_max(stream, n):
                for i, h in enumerate(HEAD_ORDER):
                    if h < QUADS:
                        wait_apart(dve, s_scores, n * HEADS + QUADS + h + 1, s_passed_dve)
                    nc.vector.tensor_tensor_reduce(out=neg_scores[:, i, :], in0=scores_ps[h], in1=penalty[stream][:],
                                                   scale=1.0, scalar=3e38, op0=ALU.add, op1=ALU.min,
                                                   accum_out=neg_max[:, h:h + 1]).then_inc(s_negmax, 1)

            def scale_oT(n):
                dve.wait_ge(s_pv, n + 1)
                dve.wait_ge(s_rT_sb, n + 1)
                nc.vector.tensor_tensor(oT[:].rearrange("p c t -> p (c t)"), oT_ps,
                                        recipT[:].rearrange("p c t -> p (c t)"), ALU.mult).then_inc(s_oT_sb, 1)

            def copy_qk(stream, m, group, half):
                dve.wait_ge(s_QK[stream], group * G + m + 1)
                if stream == "A":
                    nc.vector.tensor_copy(qkT[stream][:, m, :], half_bank[half][:]).then_inc(s_QK_sb[stream], 1)
                else:
                    nc.vector.tensor_scalar(qkT[stream][:, m, :], half_bank[half][:], bqk_col[:, m:m + 1], None,
                                            ALU.add).then_inc(s_QK_sb[stream], 1)

            def read_output(done):
                stream, b, group, n = done
                dve.wait_ge(s_out, n + 1)
                if stream == "A":
                    nc.vector.tensor_tensor(attn_out[:, b, :], out_ps, bproj_row[:], ALU.add).then_inc(s_out_read, 1)
                    dve.wait_ge(s_out_read, n + 1)
                    stats("O", attn_out[:, b, :], b, group)
                else:
                    dve.wait_ge(s_mid_bias, group * G + b + 1)
                    if not (isinstance(group, int) and group == 0):
                        dve.wait_ge(s_store[b], 16 * group)
                    nc.vector.tensor_tensor(y[:, b, :], out_ps, x_mid_bias[:, b, :], ALU.add).then_inc(s_out_read, 1)

            def slot_of(p, slot):
                done = p.finished(slot)
                if done is not None:
                    recip_of(done[3])
                    probsT_high(done[3])
                if p.active(slot):
                    mask_max(UNIT_OF_SLOT[slot][0], p.unit(slot))
                if done is not None:
                    scale_oT(done[3])
                if p.ahead and slot in (2, 3):
                    norm_in(slot - 2, p.g + 1)
                if p.a and slot in NORM_ATTN_SLOTS:
                    norm_attn(NORM_ATTN_SLOTS.index(slot), p.g)
                if p.a and slot >= 4:
                    norm_mid(slot - 4, p.g)
                for q in p.pieces(slot, 0):
                    if q[0] == "QK":
                        copy_qk(*q[1:], 0)
                if done is not None:
                    read_output(done)
                for q in p.pieces(slot, 1):
                    if q[0] == "QK":
                        copy_qk(*q[1:], 1)
                if p.ahead and slot in (1, 2):
                    for b in (2 * slot - 2, 2 * slot - 1):
                        stats_in(b, p.g + 1)
                if p.a and slot in (3, 4, 5, 6):
                    stats_mid(slot - 3, p.g)

            for b in range(G):
                stats_in(b, 0)
            dve.wait_ge(s_weights, 16 * 6)
            dve.wait_ge(s_rows, 16 * 7)
            dve.wait_ge(s_adj, 16)
            for s in "AB":
                for c in range(KC):
                    const(nc.vector.tensor_scalar(w_in[s][:, c, 0:D], w_in[s][:, c, 0:D], -SCALE, None, ALU.mult))
            const(nc.vector.tensor_scalar(bqk_col[:, 0:KC], bqk_col[:, 0:KC], -SCALE, None, ALU.mult))
            const(nc.vector.tensor_scalar(penalty["A"][:], adjacency[:], 0.0, MASKED_FIRST, ALU.is_equal, ALU.mult))
            const(nc.vector.tensor_scalar(penalty["B"][:], adjacency[:], -1.0, 1.0, ALU.mult, ALU.add))
            const(nc.vector.tensor_scalar(penalty["B"][:], penalty["B"][:], MASKED_SECOND, None, ALU.mult))
            const(nc.vector.tensor_copy(bv_wide[:], bv_col[:].unsqueeze(2).to_broadcast([128, KC, 128])))
            dve.wait_ge(s_bias_mm, 1)
            const(nc.vector.tensor_tensor(bo_row[:], out_ps, bo_row[:], ALU.add))
            assert count[0] == DVE_CONSTS
            for pair in range(2):
                norm_in(pair, 0)
            for kind, stream, i in FIRST_PIECES:
                if kind == "QK":
                    copy_qk(stream, i, 0, 0)
            each_slot(dve, slot_of)
            recip_of(END[3])
            probsT_high(END[3])
            scale_oT(END[3])
            read_output(END)


_INS = ["x", "adj", "L0_gnn_w_qkv", "L0_gnn_w_proj", "L0_gnn_b_proj", "L0_gnn_ln_gamma", "L0_gnn_ln_beta",
        "L1_gnn_Wq", "L1_gnn_bq", "L1_gnn_Wk", "L1_gnn_bk", "L1_gnn_Wv", "L1_gnn_bv", "L1_gnn_Wo", "L1_gnn_bo"]


def kernel(**inputs):
    import numpy as np
    import concourse.bacc as bacc
    from concourse.bass_utils import run_bass_kernel_spmd

    nc = bacc.Bacc("TRN2", target_bir_lowering=False, num_devices=1)
    arrays, args = {}, []
    for name in _INS:
        a = np.ascontiguousarray(inputs[name])
        arrays[f"in_{name}"] = a
        args.append(nc.dram_tensor(f"in_{name}", a.shape, mybir.dt.from_np(a.dtype), kind="ExternalInput").ap())
    args.append(nc.dram_tensor("out_x", (BATCHES, TOK, D), fp32, kind="ExternalOutput").ap())
    gnn_stack_kernel(nc, *args)
    return run_bass_kernel_spmd(nc, [arrays], core_ids=[0]).results[0]["out_x"]
```

```python
import concourse.bass as bass
from concourse import mybir
from contextlib import ExitStack

fp32 = mybir.dt.float32
fp32r = mybir.dt.float32r
ALU = mybir.AluOpType
ACT = mybir.ActivationFunctionType

BATCHES, TOK, D, HEADS = 64, 128, 256, 8
HD = D // HEADS
KC = D // 128
QUADS = 128 // HD
G = 4
GROUPS = BATCHES // G
UNITS = 2 * BATCHES
SLOTS = 8
LN_EPS = 1e-5
SCALE = float(HD) ** -0.5
MASKED_FIRST = 1e30
MASKED_SECOND = 1e9

UNIT_OF_SLOT = [(stream, b) for stream in "AB" for b in range(G)]
PIECES = [
    ([("QK", "B", 0)], [("V", "B", 0)]),
    ([("QK", "B", 1)], [("V", "B", 1)]),
    ([("QK", "B", 2)], [("T", "A", 0), ("T", "A", 1), ("V", "B", 2)]),
    ([("QK", "B", 3)], [("T", "A", 2), ("T", "A", 3), ("V", "B", 3)]),
    ([("QK", "A", 0)], [("T", "B", 0), ("V", "A", 0)]),
    ([("QK", "A", 1)], [("T", "B", 1), ("V", "A", 1)]),
    ([("QK", "A", 2)], [("T", "B", 2), ("V", "A", 2)]),
    ([("QK", "A", 3)], [("T", "B", 3), ("V", "A", 3)]),
]
NORM_ATTN_SLOTS = (2, 3, 4, 5)
OT_AFTER = 5
X_BETA_SLOTS = (3, 4, 6, 7)
FIRST_PIECES = [("T", "A", b) for b in range(G)] + [(k, "A", i) for i in range(G) for k in ("QK", "V")]


def wait_apart(engine, semaphore, value, passed):
    engine.wait_ge(semaphore, value)
    engine.sem_inc(passed, 1)


class Pass:

    def __init__(self, g, a=True, b=True, ahead=True):
        self.g, self.a, self.b, self.ahead = g, a, b, ahead
        self.first, self.last = not b, not a

    def active(self, slot):
        return self.a if UNIT_OF_SLOT[slot][0] == "A" else self.b

    def unit(self, slot):
        before = sum(self.active(s) for s in range(slot))
        if self.first:
            return before
        if self.last:
            return UNITS - G + before
        return self.g * SLOTS - G + before

    def pieces(self, slot, half):
        out = []
        for kind, stream, i in PIECES[slot][half]:
            if stream == "A" and self.ahead:
                out.append((kind, stream, i, self.g + 1))
            if stream == "B" and kind == "T" and self.a:
                out.append((kind, stream, i, self.g))
            if stream == "B" and kind != "T" and self.b:
                out.append((kind, stream, i, self.g - 1))
        return out

    def finished(self, slot):
        if slot > 0:
            if not self.active(slot - 1):
                return None
            stream, b = UNIT_OF_SLOT[slot - 1]
            return stream, b, (self.g if stream == "A" else self.g - 1), self.unit(slot - 1)
        if isinstance(self.g, int) and self.g < 2:
            return None
        return "B", G - 1, self.g - 2, self.unit(0) - 1


HEAD_ORDER = [q + QUADS * c for q in range(QUADS) for c in range(KC)]
END = ("B", G - 1, GROUPS - 1, UNITS - 1)


def each_slot(engine, slot_of):
    for slot in range(SLOTS):
        slot_of(Pass(0, b=False), slot)
    slot_of(Pass(1), 0)
    with engine.Fori(1, GROUPS - 1) as g:
        for slot in range(1, SLOTS):
            slot_of(Pass(g), slot)
        slot_of(Pass(g + 1), 0)
    for slot in range(1, SLOTS):
        slot_of(Pass(GROUPS - 1, ahead=False), slot)
    for slot in range(SLOTS):
        slot_of(Pass(GROUPS, a=False, ahead=False), slot)


def unit_of_b(b, group):
    return (group + 1) * SLOTS - G + UNIT_OF_SLOT.index(("B", b))


def gnn_stack_kernel(nc, x, adj, w_qkv, w_proj, b_proj, ln_gamma, ln_beta,
                     Wq, bq, Wk, bk, Wv, bv, Wo, bo, out):
    ctx = ExitStack()
    with ctx:
        def sb(name, shape, dt=fp32):
            return ctx.enter_context(nc.sbuf_tensor(name, shape, dt))

        def bank(name):
            return ctx.enter_context(nc.psum_tensor(name, [128, 512], fp32))

        def sem(name):
            return ctx.enter_context(nc.semaphore(name))

        def per_stream(name):
            return {"A": sem(name + "_a"), "B": sem(name + "_b")}

        w_in = {s: sb(f"w_in_{s}", [128, KC, 3 * D]) for s in "AB"}
        w_hi = {s: sb(f"w_hi_{s}", [128, KC, 3 * D], fp32r) for s in "AB"}
        w_lo = {s: sb(f"w_lo_{s}", [128, KC, 3 * D], fp32r) for s in "AB"}
        w_out = {s: sb(f"w_out_{s}", [128, KC, D]) for s in "AB"}
        adjacency = sb("adjacency", [TOK, TOK])
        penalty = {s: sb(f"penalty_{s}", [TOK, TOK]) for s in "AB"}
        ident = sb("ident", [128, 128])
        gamma_row = sb("gamma_row", [128, D])
        beta_row = sb("beta_row", [128, D])
        bproj_row = sb("bproj_row", [128, D])
        bo_row = sb("bo_row", [128, D])
        bqk_col = sb("bqk_col", [128, 2 * KC])
        bv_col = sb("bv_col", [128, KC])
        bv_wide = sb("bv_wide", [128, KC, 128])
        eps_col = sb("eps_col", [128, G])
        power_col = sb("power_col", [128, G])
        x_in = sb("x_in", [TOK, G, D])
        x_beta = sb("x_beta", [TOK, G, D])
        normed = {s: sb(f"normed_{s}", [TOK, G, D]) for s in "AB"}
        hT_hi = {s: sb(f"hT_hi_{s}", [128, KC, G * TOK], fp32r) for s in "AB"}
        hT_lo = {s: sb(f"hT_lo_{s}", [128, KC, G * TOK], fp32r) for s in "AB"}
        qkT = {s: sb(f"qkT_{s}", [128, 2 * KC, G * TOK]) for s in "AB"}
        v = {s: sb(f"v_{s}", [TOK, G, D]) for s in "AB"}
        attn_out = sb("attn_out", [TOK, G, D])
        attn_ln = sb("attn_ln", [TOK, G, D])
        x_mid = sb("x_mid", [TOK, G, D])
        x_mid_bias = sb("x_mid_bias", [TOK, G, D])
        y = sb("y", [TOK, G, D])
        moments = {s: sb(f"moments_{s}", [TOK, G, 6]) for s in "ABO"}
        mean_var = {s: sb(f"mean_var_{s}", [TOK, G, 2]) for s in "ABO"}
        var_eps = {s: sb(f"var_eps_{s}", [TOK, G]) for s in "ABO"}
        rstd = {s: sb(f"rstd_{s}", [TOK, G]) for s in "ABO"}
        neg_scores = sb("neg_scores", [TOK, HEADS, TOK])
        neg_max = sb("neg_max", [TOK, HEADS])
        probs = sb("probs", [TOK, HEADS, TOK])
        row_sum = sb("row_sum", [TOK, HEADS])
        recip = sb("recip", [TOK, HEADS])
        recip_wide = sb("recip_wide", [TOK, HEADS, HD])
        probsT = sb("probsT", [TOK, HEADS, TOK])
        recipT = sb("recipT", [128, KC, TOK])
        oT = sb("oT", [128, KC, TOK])

        head_bank = [bank(f"head_bank{j}") for j in range(QUADS)]
        half_bank = [bank(f"half_bank{j}") for j in range(2)]
        recip_out_bank = bank("recip_out_bank")
        oT_bank = bank("oT_bank")
        piece_bank = [half_bank[0], oT_bank]
        scores_ps = [head_bank[h % QUADS][:, (h // QUADS) * TOK:(h // QUADS + 1) * TOK] for h in range(HEADS)]
        rT_ps, out_ps, oT_ps = recip_out_bank[:, 0:256], recip_out_bank[:, 256:512], oT_bank[:, 0:256]

        s_weights, s_rows, s_adj = sem("weights_loaded"), sem("rows_loaded"), sem("adj_loaded")
        s_load = [sem(f"x_loaded{b}") for b in range(G)]
        s_store = [sem(f"y_stored{b}") for b in range(G)]
        s_pool_const, s_dve_const, s_bias_mm = sem("pool_consts"), sem("dve_consts"), sem("bias_product")
        s_scores, s_pT, s_rT = sem("scores_done"), sem("probsT_halves_done"), sem("recipT_done")
        s_pv, s_out = sem("pv_done"), sem("out_done")
        s_T, s_V, s_QK = per_stream("hT_done"), per_stream("v_done"), per_stream("qk_done")
        s_T_hi, s_T_sb = per_stream("hT_hi_copied"), per_stream("hT_lo_copied")
        s_V_sb, s_QK_sb = per_stream("v_copied"), per_stream("qk_copied")
        s_pT_sb = [sem("probsT_low_copied"), sem("probsT_high_copied")]
        s_rT_sb, s_oT_sb, s_out_read = sem("recipT_copied"), sem("oT_scaled"), sem("out_read")
        s_passed_dve, s_passed_sp = sem("dve_waits_passed"), sem("sp_waits_passed")
        s_negmax, s_exp, s_recip = sem("masked_with_max"), sem("exp_done"), sem("recip_done")
        s_recip_wide = sem("recip_widened")
        s_moments = {s: sem(f"moments_done_{s}") for s in "ABO"}
        s_stats = {s: sem(f"stats_done_{s}") for s in "ABO"}
        s_vareps = {s: sem(f"vareps_done_{s}") for s in "ABO"}
        s_rstd = {s: sem(f"rstd_done_{s}") for s in "ABO"}
        s_norm = {s: sem(f"normed_{s}") for s in "ABO"}
        s_mid_part = sem("x_mid_parts")
        s_mid, s_mid_bias = sem("x_mid_done"), sem("x_mid_bias_done")
        s_xbeta = sem("x_beta_done")

        block = ctx.enter_context(nc.Block())

        DVE_CONSTS = 14

        @block.sync
        def _(sp):
            def load_x(b, group):
                sp.dma_start(x_in[:, b, :], x[group * G + b, :, :]).then_inc(s_load[b], 16)

            for b in range(G):
                load_x(b, 0)
            for b in range(G):
                sp.sem_inc(s_store[b], 16)
            sp.dma_start(w_in["A"][:], w_qkv.rearrange("(c p) n -> p c n", p=128)).then_inc(s_weights, 16)
            sp.dma_start(w_out["A"][:], w_proj.rearrange("(c p) n -> p c n", p=128)).then_inc(s_weights, 16)
            sp.dma_start(adjacency[:], adj).then_inc(s_adj, 16)
            for i, w in enumerate((Wq, Wk, Wv)):
                sp.dma_start(w_in["B"][:, :, i * D:(i + 1) * D],
                             w.rearrange("(c p) n -> p c n", p=128)).then_inc(s_weights, 16)
            sp.dma_start(w_out["B"][:], Wo.rearrange("(c p) n -> p c n", p=128)).then_inc(s_weights, 16)
            for t, row in ((gamma_row, ln_gamma), (beta_row, ln_beta), (bproj_row, b_proj), (bo_row, bo)):
                sp.dma_start(t[:], row.rearrange("(a n) -> a n", a=1).broadcast_to([128, D])).then_inc(s_rows, 16)
            with nc.allow_non_contiguous_dma(reason="bias columns, 256 floats each"):
                for t, col in ((bqk_col[:, 0:KC], bq), (bqk_col[:, KC:2 * KC], bk), (bv_col[:], bv)):
                    sp.dma_start(t, col.rearrange("(c p) -> p c", p=128)).then_inc(s_rows, 16)

            def store(unit):
                if unit is not None and unit[0] == "B":
                    _, b, group, n = unit
                    wait_apart(sp, s_out_read, n + 1, s_passed_sp)
                    sp.dma_start(out[group * G + b, :, :], y[:, b, :]).then_inc(s_store[b], 16)

            def slot_of(p, slot):
                if p.ahead and slot == 1:
                    for b in range(G):
                        wait_apart(sp, s_norm["A"], (p.g + 1) * G, s_passed_sp)
                        wait_apart(sp, s_xbeta, p.g * G + b + 1, s_passed_sp)
                        load_x(b, p.g + 1)
                store(p.finished(slot))

            each_slot(sp, slot_of)
            store(END)
            for b in range(G):
                sp.wait_ge(s_store[b], 16 * (GROUPS + 1))

        @block.gpsimd
        def _(pool):
            nc.gpsimd.memset(ident[:], 0.0).then_inc(s_pool_const, 1)
            nc.gpsimd.memset(eps_col[:], LN_EPS).then_inc(s_pool_const, 1)
            nc.gpsimd.memset(power_col[:], -0.5).then_inc(s_pool_const, 1)
            pool.wait_ge(s_pool_const, 3)
            nc.gpsimd.affine_select(out=ident[:], in_=ident[:], compare_op=ALU.not_equal, fill=1.0, base=0,
                                    pattern=[[-1, 128]], channel_multiplier=1).then_inc(s_pool_const, 1)

            def rstd_of(kind, b0, n, group):
                count = group * (G // n) + b0 // n + 1
                pool.wait_ge(s_stats[kind], group * G + b0 + n)
                nc.gpsimd.tensor_tensor(var_eps[kind][:, b0:b0 + n], mean_var[kind][:, b0:b0 + n, 1],
                                        eps_col[:, 0:n], ALU.add).then_inc(s_vareps[kind], 1)
                pool.wait_ge(s_vareps[kind], count)
                nc.gpsimd.tensor_tensor(rstd[kind][:, b0:b0 + n], var_eps[kind][:, b0:b0 + n],
                                        power_col[:, 0:n], ALU.pow).then_inc(s_rstd[kind], 1)

            def x_beta_of(b, group):
                pool.wait_ge(s_load[b], (group + 1) * 16)
                if not (isinstance(group, int) and group == 0):
                    pool.wait_ge(s_mid, (group - 1) * G + b + 1)
                nc.gpsimd.tensor_tensor(x_beta[:, b, :], x_in[:, b, :], beta_row[:], ALU.add).then_inc(s_xbeta, 1)

            def x_mid_of(b, group):
                done = (group * G + b) * 2
                pool.wait_ge(s_norm["O"], group * G + b + 1)
                nc.gpsimd.tensor_tensor(attn_ln[:, b, :], attn_ln[:, b, :], gamma_row[:],
                                        ALU.mult).then_inc(s_mid_part, 1)
                pool.wait_ge(s_mid_part, done + 1)
                nc.gpsimd.tensor_tensor(attn_out[:, b, :], attn_out[:, b, :], attn_ln[:, b, :],
                                        ALU.add).then_inc(s_mid_part, 1)
                pool.wait_ge(s_mid_part, done + 2)
                pool.wait_ge(s_xbeta, group * G + b + 1)
                nc.gpsimd.tensor_tensor(x_mid[:, b, :], attn_out[:, b, :], x_beta[:, b, :],
                                        ALU.add).then_inc(s_mid, 1)

            def x_mid_bias_of(b, group):
                pool.wait_ge(s_mid, group * G + b + 1)
                if not (isinstance(group, int) and group == 0):
                    pool.wait_ge(s_out_read, unit_of_b(b, group - 1) + 1)
                nc.gpsimd.tensor_tensor(x_mid_bias[:, b, :], x_mid[:, b, :], bo_row[:],
                                        ALU.add).then_inc(s_mid_bias, 1)

            pool.wait_ge(s_rows, 16 * 7)
            for b in range(0, G, 2):
                rstd_of("A", b, 2, 0)
            for b in range(G):
                x_beta_of(b, 0)
            pool.wait_ge(s_dve_const, DVE_CONSTS)

            def slot_of(p, slot):
                if p.a and 4 <= slot:
                    rstd_of("B", slot - 4, 1, p.g)
                if p.ahead and slot in (2, 3):
                    rstd_of("A", 2 * (slot - 2), 2, p.g + 1)
                if p.a and slot in NORM_ATTN_SLOTS:
                    b = NORM_ATTN_SLOTS.index(slot)
                    rstd_of("O", b, 1, p.g)
                    x_mid_of(b, p.g)
                if p.ahead and slot in X_BETA_SLOTS:
                    x_beta_of(X_BETA_SLOTS.index(slot), p.g + 1)
                if slot == 0 and p.b:
                    x_mid_bias_of(2, p.g - 1)
                if slot == 1 and p.b:
                    x_mid_bias_of(3, p.g - 1)
                if slot == 5 and p.a:
                    x_mid_bias_of(0, p.g)
                if slot == 7 and p.a:
                    x_mid_bias_of(1, p.g)

            each_slot(pool, slot_of)

        @block.tensor
        def _(pe):
            copied = {"T": s_T_sb, "V": s_V_sb, "QK": s_QK_sb}

            def transposed_h(stream, b, group, units):
                pe.wait_ge(s_norm[stream], group * G + b + 1)
                if units is not None:
                    pe.wait_ge(s_negmax, units * HEADS)
                for c in range(KC):
                    mm = nc.tensor.transpose(head_bank[b][:, c * 128:(c + 1) * 128],
                                             normed[stream][:, b, c * 128:(c + 1) * 128], ident[:])
                mm.then_inc(s_T[stream], 1)

            def parts(a_hi, a_lo, b_hi, b_lo):
                return (a_hi, b_hi), (a_hi, b_lo), (a_lo, b_hi)

            def values(stream, b, group, bank):
                pe.wait_ge(s_T_sb[stream], group * G + b + 1)
                for t, (h, w) in enumerate(parts(hT_hi[stream], hT_lo[stream], w_hi[stream], w_lo[stream])):
                    for c in range(KC):
                        mm = nc.tensor.matmul(bank[:, 0:D], h[:, c, b * TOK:(b + 1) * TOK], w[:, c, 2 * D:3 * D],
                                              start=(t == 0 and c == 0), stop=(t == 2 and c == KC - 1))
                mm.then_inc(s_V[stream], 1)

            def queries_keys(stream, m, group, bank):
                pe.wait_ge(s_T_sb[stream], (group + 1) * G)
                for t, (h, w) in enumerate(parts(hT_hi[stream], hT_lo[stream], w_hi[stream], w_lo[stream])):
                    for c in range(KC):
                        mm = nc.tensor.matmul(bank[:], w[:, c, m * 128:(m + 1) * 128], h[:, c, :],
                                              start=(t == 0 and c == 0), stop=(t == 2 and c == KC - 1))
                mm.then_inc(s_QK[stream], 1)

            def piece_before_copied(p, slot, half):
                if slot > 0:
                    for kind, stream, i, group in p.pieces(slot - 1, half):
                        if kind != "T":
                            pe.wait_ge(copied[kind][stream], group * G + i + 1)
                elif not p.last:
                    pe.wait_ge((s_QK_sb, s_V_sb)[half]["A"], (p.g + 1) * G)

            def pieces(p, slot, half, done):
                for kind, stream, i, group in p.pieces(slot, half):
                    if kind == "T":
                        transposed_h(stream, i, group, p.unit(slot) + p.active(slot))
                        continue
                    bank = piece_bank[half]
                    if done is None:
                        piece_before_copied(p, slot, half)
                    elif half == 0:
                        pe.wait_ge(s_pT_sb[0], done[3] + 1)
                    else:
                        pe.wait_ge(s_oT_sb, done[3] + 1)
                    (values if kind == "V" else queries_keys)(stream, i, group, bank)

            def scores(stream, b, group, n, p, slot):
                if b == 0:
                    pe.wait_ge(s_QK_sb[stream], (group + 1) * G)
                if not (p.first and slot == 0):
                    pe.wait_ge(s_negmax, n * HEADS)
                if slot > 0:
                    transposes = [q for half in range(2) for q in p.pieces(slot - 1, half) if q[0] == "T"]
                    for _, last_stream, last, its_group in transposes[-1:]:
                        pe.wait_ge(s_T_sb[last_stream], its_group * G + last + 1)
                elif not p.first:
                    pe.wait_ge(s_T_sb["B"], p.g * G)
                tokens = slice(b * TOK, (b + 1) * TOK)
                for h in range(HEADS):
                    c, lanes = h // QUADS, slice(HD * (h % QUADS), HD * (h % QUADS + 1))
                    nc.tensor.matmul(scores_ps[h], qkT[stream][lanes, c, tokens],
                                     qkT[stream][lanes, KC + c, tokens],
                                     start=True, stop=True).then_inc(s_scores, 1)

            def transposed_probs(n, p, slot):
                first = p is not None and p.first and slot == 1
                for half in range(2):
                    pe.wait_ge(s_exp, n * HEADS + 4 * (half + 1))
                    if not first:
                        pe.wait_ge(s_pT_sb[half], n)
                    if p is not None and half == 0:
                        piece_before_copied(p, slot, 0)
                    for i in range(4):
                        mm = nc.tensor.transpose(half_bank[half][:, i * TOK:(i + 1) * TOK],
                                                 probs[:, 4 * half + i, :], ident[:])
                    mm.then_inc(s_pT, 1)
                pe.wait_ge(s_recip_wide, n + 1)
                if not first:
                    pe.wait_ge(s_out_read, n)
                for c in range(KC):
                    mm = nc.tensor.transpose(rT_ps[:, c * TOK:(c + 1) * TOK],
                                             recip_wide[:, c * QUADS:(c + 1) * QUADS, :].rearrange("p h d -> p (h d)"),
                                             ident[:])
                mm.then_inc(s_rT, 1)

            def probs_values(stream, b, group, n, p, slot):
                pe.wait_ge(s_V_sb[stream], group * G + b + 1)
                if p is not None:
                    piece_before_copied(p, slot, 1)
                for half in range(2):
                    pe.wait_ge(s_pT_sb[half], n + 1)
                    if half == 0 and not (isinstance(n, int) and n == 0):
                        pe.wait_ge(s_oT_sb, n)
                    for i in range(4 * half, 4 * half + 4):
                        h = HEAD_ORDER[i]
                        c, lanes = h // QUADS, slice(HD * (h % QUADS), HD * (h % QUADS + 1))
                        mm = nc.tensor.matmul(oT_ps[lanes, c * TOK:(c + 1) * TOK],
                                              v[stream][:, b, h * HD:(h + 1) * HD],
                                              probsT[:, i, :], start=True, stop=True, skip_group_check=True)
                mm.then_inc(s_pv, 1)

            def output(stream, n):
                pe.wait_ge(s_oT_sb, n + 1)
                pe.wait_ge(s_rT_sb, n + 1)
                for c in range(KC):
                    mm = nc.tensor.matmul(out_ps, oT[:, c, :], w_out[stream][:, c, :],
                                          start=(c == 0), stop=(c == KC - 1))
                mm.then_inc(s_out, 1)

            def slot_of(p, slot):
                done = p.finished(slot)
                if done is not None:
                    transposed_probs(done[3], p, slot)
                if p.active(slot):
                    stream, b = UNIT_OF_SLOT[slot]
                    scores(stream, b, p.g if stream == "A" else p.g - 1, p.unit(slot), p, slot)
                if done is not None:
                    probs_values(*done, p, slot)
                pieces(p, slot, 0, done)
                if done is not None:
                    output(done[0], done[3])
                pieces(p, slot, 1, done)

            pe.wait_ge(s_pool_const, 4)
            pe.wait_ge(s_dve_const, DVE_CONSTS - 1)
            for c in range(KC):
                mm = nc.tensor.matmul(out_ps, bv_wide[:, c, :], w_out["B"][:, c, :], start=(c == 0), stop=(c == KC - 1))
            mm.then_inc(s_bias_mm, 1)
            pe.wait_ge(s_dve_const, DVE_CONSTS)
            for kind, stream, i in FIRST_PIECES:
                if kind == "T":
                    transposed_h(stream, i, 0, None)
                    continue
                if i > 0:
                    pe.wait_ge(copied[kind][stream], i)
                if kind == "QK":
                    queries_keys(stream, i, 0, half_bank[0])
                else:
                    values(stream, i, 0, piece_bank[1])
            each_slot(pe, slot_of)
            transposed_probs(END[3], None, None)
            probs_values(*END, None, None)
            output(END[0], END[3])

        @block.scalar
        def _(act):
            def copy_piece(kind, stream, i, group, half):
                if kind == "T":
                    act.wait_ge(s_T[stream], group * G + i + 1)
                    nc.scalar.activation(hT_hi[stream][:, :, i * TOK:(i + 1) * TOK],
                                         head_bank[i][:, 0:256].rearrange("p (c t) -> p c t", c=KC),
                                         ACT.Relu).then_inc(s_T_hi[stream], 1)
                if kind == "V":
                    act.wait_ge(s_V[stream], group * G + i + 1)
                    nc.scalar.copy(v[stream][:, i, :], piece_bank[half][:, 0:D]).then_inc(s_V_sb[stream], 1)

            def tail(done):
                n = done[3]
                act.wait_ge(s_pT, 2 * n + 1)
                nc.scalar.copy(probsT[:, 0:4, :].rearrange("p h t -> p (h t)"), half_bank[0][:]).then_inc(s_pT_sb[0], 1)
                act.wait_ge(s_rT, n + 1)
                nc.scalar.copy(recipT[:].rearrange("p c t -> p (c t)"), rT_ps).then_inc(s_rT_sb, 1)

            def exps(n):
                for i, h in enumerate(HEAD_ORDER):
                    act.wait_ge(s_negmax, n * HEADS + i + 1)
                    nc.scalar.activation(probs[:, i, :], neg_scores[:, i, :], ACT.Exp, scale=-1.0,
                                         bias=neg_max[:, h:h + 1], accum_out=row_sum[:, h:h + 1]).then_inc(s_exp, 1)

            def slot_of(p, slot):
                done = p.finished(slot)
                if done is not None:
                    tail(done)
                if p.active(slot):
                    exps(p.unit(slot))
                for half in range(2):
                    for q in p.pieces(slot, half):
                        copy_piece(*q, half)

            for q in FIRST_PIECES:
                copy_piece(*q, 0, 1)
            each_slot(act, slot_of)
            tail(END)

        @block.vector
        def _(dve):
            count = [0]

            def const(ins):
                count[0] += 1
                ins.then_inc(s_dve_const, 1)
                dve.wait_ge(s_dve_const, count[0])

            def stats(kind, source, b, group):
                nc.vector.bn_stats(moments[kind][:, b, :], source).then_inc(s_moments[kind], 1)
                wait_apart(dve, s_moments[kind], group * G + b + 1, s_passed_dve)
                nc.vector.bn_aggr(mean_var[kind][:, b, :], moments[kind][:, b, :]).then_inc(s_stats[kind], 1)

            def stats_in(b, group):
                dve.wait_ge(s_load[b], (group + 1) * 16)
                stats("A", x_in[:, b, :], b, group)

            def stats_mid(b, group):
                dve.wait_ge(s_mid, group * G + b + 1)
                stats("B", x_mid[:, b, :], b, group)

            def norm(kind, target, source, b, group):
                nc.vector.tensor_scalar(target[:, b, :], source[:, b, :], mean_var[kind][:, b, 0:1],
                                        rstd[kind][:, b:b + 1], ALU.subtract, ALU.mult).then_inc(s_norm[kind], 1)

            def norm_in(pair, group):
                dve.wait_ge(s_rstd["A"], group * 2 + pair + 1)
                for b in (2 * pair, 2 * pair + 1):
                    norm("A", normed["A"], x_in, b, group)

            def norm_mid(b, group):
                dve.wait_ge(s_rstd["B"], group * G + b + 1)
                norm("B", normed["B"], x_mid, b, group)

            def norm_attn(b, group):
                dve.wait_ge(s_rstd["O"], group * G + b + 1)
                norm("O", attn_ln, attn_out, b, group)

            def recip_of(n):
                dve.wait_ge(s_exp, (n + 1) * HEADS)
                nc.vector.reciprocal(recip[:], row_sum[:]).then_inc(s_recip, 1)
                dve.wait_ge(s_recip, n + 1)
                nc.vector.tensor_copy(recip_wide[:],
                                      recip[:].unsqueeze(2).to_broadcast([TOK, HEADS, HD])).then_inc(s_recip_wide, 1)

            def probsT_high(n):
                dve.wait_ge(s_pT, 2 * n + 2)
                nc.vector.tensor_copy(probsT[:, 4:8, :].rearrange("p h t -> p (h t)"),
                                      half_bank[1][:]).then_inc(s_pT_sb[1], 1)

            def mask_max(stream, n, heads):
                for i in heads:
                    h = HEAD_ORDER[i]
                    if h < QUADS:
                        wait_apart(dve, s_scores, n * HEADS + QUADS + h + 1, s_passed_dve)
                    nc.vector.tensor_tensor_reduce(out=neg_scores[:, i, :], in0=scores_ps[h], in1=penalty[stream][:],
                                                   scale=1.0, scalar=3e38, op0=ALU.add, op1=ALU.min,
                                                   accum_out=neg_max[:, h:h + 1]).then_inc(s_negmax, 1)

            def scale_oT(n):
                dve.wait_ge(s_pv, n + 1)
                dve.wait_ge(s_rT_sb, n + 1)
                nc.vector.tensor_tensor(oT[:].rearrange("p c t -> p (c t)"), oT_ps,
                                        recipT[:].rearrange("p c t -> p (c t)"), ALU.mult).then_inc(s_oT_sb, 1)

            def copy_qk(stream, m, group, half):
                dve.wait_ge(s_QK[stream], group * G + m + 1)
                if stream == "A":
                    nc.vector.tensor_copy(qkT[stream][:, m, :], piece_bank[half][:]).then_inc(s_QK_sb[stream], 1)
                else:
                    nc.vector.tensor_scalar(qkT[stream][:, m, :], piece_bank[half][:], bqk_col[:, m:m + 1], None,
                                            ALU.add).then_inc(s_QK_sb[stream], 1)

            def hT_rest(stream, b, group):
                dve.wait_ge(s_T_hi[stream], group * G + b + 1)
                tokens = slice(b * TOK, (b + 1) * TOK)
                nc.vector.scalar_tensor_tensor(
                    out=hT_lo[stream][:, :, tokens], in0=head_bank[b][:, 0:256].rearrange("p (c t) -> p c t", c=KC),
                    scalar=0.0, in1=hT_hi[stream][:, :, tokens].bitcast(fp32),
                    op0=ALU.max, op1=ALU.subtract).then_inc(s_T_sb[stream], 1)

            def read_output(done):
                stream, b, group, n = done
                dve.wait_ge(s_out, n + 1)
                if stream == "A":
                    nc.vector.tensor_tensor(attn_out[:, b, :], out_ps, bproj_row[:], ALU.add).then_inc(s_out_read, 1)
                    dve.wait_ge(s_out_read, n + 1)
                    stats("O", attn_out[:, b, :], b, group)
                else:
                    dve.wait_ge(s_mid_bias, group * G + b + 1)
                    dve.wait_ge(s_store[b], 16 * (group + 1))
                    nc.vector.tensor_tensor(y[:, b, :], out_ps, x_mid_bias[:, b, :], ALU.add).then_inc(s_out_read, 1)

            def slot_of(p, slot):
                done = p.finished(slot)
                if done is not None:
                    probsT_high(done[3])
                if p.active(slot):
                    mask_max(UNIT_OF_SLOT[slot][0], p.unit(slot), range(OT_AFTER))
                if done is not None:
                    scale_oT(done[3])
                if p.active(slot):
                    mask_max(UNIT_OF_SLOT[slot][0], p.unit(slot), range(OT_AFTER, HEADS))
                if p.ahead and slot in (2, 3):
                    norm_in(slot - 2, p.g + 1)
                if p.a and slot in NORM_ATTN_SLOTS:
                    norm_attn(NORM_ATTN_SLOTS.index(slot), p.g)
                if p.a and slot >= 4:
                    norm_mid(slot - 4, p.g)
                for q in p.pieces(slot, 0):
                    if q[0] == "QK":
                        copy_qk(*q[1:], 0)
                if p.active(slot):
                    recip_of(p.unit(slot))
                if done is not None:
                    read_output(done)
                for q in p.pieces(slot, 1):
                    if q[0] == "T":
                        hT_rest(*q[1:])
                    if q[0] == "QK":
                        copy_qk(*q[1:], 1)
                if p.ahead and slot in (1, 2):
                    for b in (2 * slot - 2, 2 * slot - 1):
                        stats_in(b, p.g + 1)
                if p.a and slot in (3, 4, 5, 6):
                    stats_mid(slot - 3, p.g)

            for b in range(G):
                stats_in(b, 0)
            dve.wait_ge(s_weights, 16 * 6)
            dve.wait_ge(s_rows, 16 * 7)
            dve.wait_ge(s_adj, 16)
            for s in "AB":
                for c in range(KC):
                    const(nc.vector.tensor_scalar(w_in[s][:, c, 0:D], w_in[s][:, c, 0:D], -SCALE, None, ALU.mult))
            for s in "AB":
                const(nc.vector.tensor_copy(w_hi[s][:], w_in[s][:]))
                const(nc.vector.tensor_tensor(w_lo[s][:], w_in[s][:], w_hi[s][:].bitcast(fp32), ALU.subtract))
            const(nc.vector.tensor_scalar(bqk_col[:, 0:KC], bqk_col[:, 0:KC], -SCALE, None, ALU.mult))
            const(nc.vector.tensor_scalar(penalty["A"][:], adjacency[:], 0.0, MASKED_FIRST, ALU.is_equal, ALU.mult))
            const(nc.vector.tensor_scalar(penalty["B"][:], adjacency[:], -1.0, 1.0, ALU.mult, ALU.add))
            const(nc.vector.tensor_scalar(penalty["B"][:], penalty["B"][:], MASKED_SECOND, None, ALU.mult))
            const(nc.vector.tensor_copy(bv_wide[:], bv_col[:].unsqueeze(2).to_broadcast([128, KC, 128])))
            dve.wait_ge(s_bias_mm, 1)
            const(nc.vector.tensor_tensor(bo_row[:], out_ps, bo_row[:], ALU.add))
            assert count[0] == DVE_CONSTS
            for pair in range(2):
                norm_in(pair, 0)
            for kind, stream, i in FIRST_PIECES:
                if kind == "T":
                    hT_rest(stream, i, 0)
                if kind == "QK":
                    copy_qk(stream, i, 0, 0)
            each_slot(dve, slot_of)
            probsT_high(END[3])
            scale_oT(END[3])
            read_output(END)


_INS = ["x", "adj", "L0_gnn_w_qkv", "L0_gnn_w_proj", "L0_gnn_b_proj", "L0_gnn_ln_gamma", "L0_gnn_ln_beta",
        "L1_gnn_Wq", "L1_gnn_bq", "L1_gnn_Wk", "L1_gnn_bk", "L1_gnn_Wv", "L1_gnn_bv", "L1_gnn_Wo", "L1_gnn_bo"]


def kernel(**inputs):
    import numpy as np
    import concourse.bacc as bacc
    from concourse.bass_utils import run_bass_kernel_spmd

    nc = bacc.Bacc("TRN2", target_bir_lowering=False, num_devices=1)
    arrays, args = {}, []
    for name in _INS:
        a = np.ascontiguousarray(inputs[name])
        arrays[f"in_{name}"] = a
        args.append(nc.dram_tensor(f"in_{name}", a.shape, mybir.dt.from_np(a.dtype), kind="ExternalInput").ap())
    args.append(nc.dram_tensor("out_x", (BATCHES, TOK, D), fp32, kind="ExternalOutput").ap())
    gnn_stack_kernel(nc, *args)
    return run_bass_kernel_spmd(nc, [arrays], core_ids=[0]).results[0]["out_x"]
```

```python
import concourse.bass as bass
from concourse import mybir
from contextlib import ExitStack

fp32 = mybir.dt.float32
fp32r = mybir.dt.float32r
ALU = mybir.AluOpType
ACT = mybir.ActivationFunctionType

BATCHES, TOK, D, HEADS = 64, 128, 256, 8
HD = D // HEADS
KC = D // 128
QUADS = 128 // HD
G = 4
GROUPS = BATCHES // G
UNITS = 2 * BATCHES
SLOTS = 8
LN_EPS = 1e-5
SCALE = float(HD) ** -0.5
MASKED_FIRST = 1e30
MASKED_SECOND = 1e9

UNIT_OF_SLOT = [(stream, b) for stream in "AB" for b in range(G)]
PIECES = [[("V", "A", i), ("T", "A", i), ("QK", "B", i)] for i in range(G)] + \
         [[("V", "B", i), ("T", "B", i), ("QK", "A", i)] for i in range(G)]
RECIP_AFTER, WIDEN_AFTER = 2, 3
OUT_AFTER, NORM_AFTER = 4, 5
TAIL_AFTER, COPIES_AFTER = 4, 6
X_MID_SLOTS = (3, 4, 5, 6)
X_BETA_SLOTS = (5, 6, 7, 7)
FIRST_PIECES = [(kind, "A", i) for kind in ("T", "QK") for i in range(G)]


def wait_apart(engine, semaphore, value, passed):
    engine.wait_ge(semaphore, value)
    engine.sem_inc(passed, 1)


class Pass:

    def __init__(self, g, a=True, b=True, ahead=True, load=True):
        self.g, self.a, self.b, self.ahead, self.load = g, a, b, ahead, load
        self.first, self.last = not b, not a

    def active(self, slot):
        return self.a if UNIT_OF_SLOT[slot][0] == "A" else self.b

    def unit(self, slot):
        before = sum(self.active(s) for s in range(slot))
        if self.first:
            return before
        if self.last:
            return UNITS - G + before
        return self.g * SLOTS - G + before

    def pieces(self, slot):
        exists = {("V", "A"): self.a, ("V", "B"): self.b, ("T", "A"): self.ahead, ("T", "B"): self.a,
                  ("QK", "A"): self.ahead, ("QK", "B"): self.b}
        group = {("V", "A"): self.g, ("V", "B"): self.g - 1, ("T", "A"): self.g + 1, ("T", "B"): self.g,
                 ("QK", "A"): self.g + 1, ("QK", "B"): self.g - 1}
        return [(kind, stream, i, group[kind, stream]) for kind, stream, i in PIECES[slot] if exists[kind, stream]]

    def piece(self, slot, kind):
        for its_kind, stream, i, group in self.pieces(slot):
            if its_kind == kind:
                return stream, i, group

    def before(self, slot, back):
        at = slot - back
        if at >= 0:
            if not self.active(at):
                return None
            stream, b = UNIT_OF_SLOT[at]
            return stream, b, (self.g if stream == "A" else self.g - 1), self.unit(at)
        if isinstance(self.g, int) and self.g < 2:
            return None
        return "B", G + at, self.g - 2, self.unit(0) + at


HEAD_ORDER = [q + QUADS * c for q in range(QUADS) for c in range(KC)]
LAST = [("B", b, GROUPS - 1, UNITS - G + b) for b in (G - 2, G - 1)]


def each_slot(engine, slot_of):
    for slot in range(SLOTS):
        slot_of(Pass(0, b=False), slot)
    for slot in range(2):
        slot_of(Pass(1), slot)
    with engine.Fori(1, GROUPS - 2) as g:
        for slot in range(2, SLOTS):
            slot_of(Pass(g), slot)
        for slot in range(2):
            slot_of(Pass(g + 1), slot)
    for slot in range(2, SLOTS):
        slot_of(Pass(GROUPS - 2, load=False), slot)
    for slot in range(SLOTS):
        slot_of(Pass(GROUPS - 1, ahead=False, load=False), slot)
    for slot in range(SLOTS):
        slot_of(Pass(GROUPS, a=False, ahead=False, load=False), slot)


def unit_of_b(b, group):
    return (group + 1) * SLOTS - G + UNIT_OF_SLOT.index(("B", b))


def gnn_stack_kernel(nc, x, adj, w_qkv, w_proj, b_proj, ln_gamma, ln_beta,
                     Wq, bq, Wk, bk, Wv, bv, Wo, bo, out):
    ctx = ExitStack()
    with ctx:
        def sb(name, shape, dt=fp32):
            return ctx.enter_context(nc.sbuf_tensor(name, shape, dt))

        def bank(name):
            return ctx.enter_context(nc.psum_tensor(name, [128, 512], fp32))

        def sem(name):
            return ctx.enter_context(nc.semaphore(name))

        def per_stream(name):
            return {"A": sem(name + "_a"), "B": sem(name + "_b")}

        w_in = {s: sb(f"w_in_{s}", [128, KC, 3 * D]) for s in "AB"}
        w_hi = {s: sb(f"w_hi_{s}", [128, KC, 3 * D], fp32r) for s in "AB"}
        w_lo = {s: sb(f"w_lo_{s}", [128, KC, 3 * D], fp32r) for s in "AB"}
        w_out = {s: sb(f"w_out_{s}", [128, KC, D]) for s in "AB"}
        w_out_hi = {s: sb(f"w_out_hi_{s}", [128, KC, D], fp32r) for s in "AB"}
        w_out_lo = {s: sb(f"w_out_lo_{s}", [128, KC, D], fp32r) for s in "AB"}
        adjacency = sb("adjacency", [TOK, TOK])
        penalty = {s: sb(f"penalty_{s}", [TOK, TOK]) for s in "AB"}
        ident = sb("ident", [128, 128])
        gamma_row = sb("gamma_row", [128, D])
        beta_row = sb("beta_row", [128, D])
        bproj_row = sb("bproj_row", [128, D])
        bo_row = sb("bo_row", [128, D])
        bqk_col = sb("bqk_col", [128, 2 * KC])
        bv_col = sb("bv_col", [128, KC])
        bv_wide = sb("bv_wide", [128, KC, 128])
        eps_col = sb("eps_col", [128, G])
        power_col = sb("power_col", [128, G])
        x_in = sb("x_in", [TOK, G, D])
        x_beta = sb("x_beta", [TOK, G, D])
        normed = {s: sb(f"normed_{s}", [TOK, G, D]) for s in "AB"}
        hT_hi = {s: sb(f"hT_hi_{s}", [128, KC, G * TOK], fp32r) for s in "AB"}
        hT_lo = {s: sb(f"hT_lo_{s}", [128, KC, G * TOK], fp32r) for s in "AB"}
        qkT = {s: sb(f"qkT_{s}", [128, 2 * KC, G * TOK]) for s in "AB"}
        v = {s: sb(f"v_{s}", [TOK, G, D]) for s in "AB"}
        attn_out = sb("attn_out", [TOK, G, D])
        attn_ln = sb("attn_ln", [TOK, G, D])
        x_mid = sb("x_mid", [TOK, G, D])
        x_mid_bias = sb("x_mid_bias", [TOK, G, D])
        y = sb("y", [TOK, G, D])
        moments = {s: sb(f"moments_{s}", [TOK, G, 6]) for s in "ABO"}
        mean_var = {s: sb(f"mean_var_{s}", [TOK, G, 2]) for s in "ABO"}
        var_eps = {s: sb(f"var_eps_{s}", [TOK, G]) for s in "ABO"}
        rstd = {s: sb(f"rstd_{s}", [TOK, G]) for s in "ABO"}
        neg_scores = [sb(f"neg_scores{i}", [TOK, HEADS, TOK]) for i in range(2)]
        neg_max = [sb(f"neg_max{i}", [TOK, HEADS]) for i in range(2)]
        probs = [sb(f"probs{i}", [TOK, HEADS, TOK]) for i in range(2)]
        row_sum = [sb(f"row_sum{i}", [TOK, HEADS]) for i in range(2)]
        recip = sb("recip", [TOK, HEADS])
        recip_wide = sb("recip_wide", [TOK, HEADS, HD])
        probsT = sb("probsT", [TOK, HEADS, TOK])
        recipT = sb("recipT", [128, KC, TOK])
        oT = sb("oT", [128, KC, TOK])
        oT_hi = sb("oT_hi", [128, KC, TOK], fp32r)
        oT_lo = sb("oT_lo", [128, KC, TOK], fp32r)

        head_bank = [bank(f"head_bank{j}") for j in range(QUADS)]
        half_bank = [bank(f"half_bank{j}") for j in range(2)]
        recip_out_bank = bank("recip_out_bank")
        oT_bank = bank("oT_bank")
        PIECE_BANK = {"T": head_bank[0], "V": oT_bank}

        def qk_bank(p, slot):
            return half_bank[slot % 2 if p.last else 0]

        scores_ps = [head_bank[h % QUADS][:, (h // QUADS) * TOK:(h // QUADS + 1) * TOK] for h in range(HEADS)]
        rT_ps, out_ps, oT_ps = recip_out_bank[:, 0:256], recip_out_bank[:, 256:512], oT_bank[:, 0:256]

        s_w_in, s_w_out = per_stream("w_in_loaded"), per_stream("w_out_loaded")
        s_rows, s_cols, s_adj = sem("rows_loaded"), sem("cols_loaded"), sem("adj_loaded")
        s_load = [sem(f"x_loaded{b}") for b in range(G)]
        s_store = [sem(f"y_stored{b}") for b in range(G)]
        s_pool_const, s_dve_const, s_bias_mm = sem("pool_consts"), sem("dve_consts"), sem("bias_product")
        s_w_hi, s_w_lo = per_stream("w_hi_blocks"), per_stream("w_lo_blocks")
        s_scores, s_pT, s_rT = sem("scores_done"), sem("probsT_halves_done"), sem("recipT_done")
        s_pv, s_out = sem("pv_done"), sem("out_done")
        s_T, s_V, s_QK = per_stream("hT_done"), per_stream("v_done"), per_stream("qk_done")
        s_T_hi, s_T_sb = per_stream("hT_hi_copied"), per_stream("hT_lo_copied")
        s_V_sb, s_QK_sb = per_stream("v_copied"), per_stream("qk_copied")
        s_pT_sb = [sem("probsT_low_copied"), sem("probsT_high_copied")]
        s_rT_sb, s_oT_sb, s_out_read = sem("recipT_copied"), sem("oT_scaled"), sem("out_read")
        s_oT_hi, s_oT_lo = sem("oT_hi_done"), sem("oT_lo_done")
        s_passed_dve, s_passed_sp = sem("dve_waits_passed"), sem("sp_waits_passed")
        s_negmax, s_exp, s_recip = sem("masked_with_max"), sem("exp_done"), sem("recip_done")
        s_recip_wide = sem("recip_widened")
        s_moments = {s: sem(f"moments_done_{s}") for s in "ABO"}
        s_stats = {s: sem(f"stats_done_{s}") for s in "ABO"}
        s_vareps = {s: sem(f"vareps_done_{s}") for s in "ABO"}
        s_rstd = {s: sem(f"rstd_done_{s}") for s in "ABO"}
        s_norm = {s: sem(f"normed_{s}") for s in "ABO"}
        s_mid_part = sem("x_mid_parts")
        s_mid, s_mid_bias = sem("x_mid_done"), sem("x_mid_bias_done")
        s_xbeta = sem("x_beta_done")

        block = ctx.enter_context(nc.Block())

        DVE_CONSTS = 4

        @block.sync
        def _(sp):
            def load_x(b, group):
                sp.dma_start(x_in[:, b, :], x[group * G + b, :, :]).then_inc(s_load[b], 16)

            def row(target, source):
                sp.dma_start(target[:], source.rearrange("(a n) -> a n", a=1).broadcast_to([128, D])).then_inc(s_rows, 16)

            for b in range(G):
                load_x(b, 0)
            sp.dma_start(w_in["A"][:], w_qkv.rearrange("(c p) n -> p c n", p=128)).then_inc(s_w_in["A"], 16)
            sp.dma_start(adjacency[:], adj).then_inc(s_adj, 16)
            for i, w in enumerate((Wq, Wk, Wv)):
                sp.dma_start(w_in["B"][:, :, i * D:(i + 1) * D],
                             w.rearrange("(c p) n -> p c n", p=128)).then_inc(s_w_in["B"], 16)
            sp.dma_start(w_out["B"][:], Wo.rearrange("(c p) n -> p c n", p=128)).then_inc(s_w_out["B"], 16)
            with nc.allow_non_contiguous_dma(reason="bias columns, 256 floats each"):
                for t, col in ((bqk_col[:, 0:KC], bq), (bqk_col[:, KC:2 * KC], bk), (bv_col[:], bv)):
                    sp.dma_start(t, col.rearrange("(c p) -> p c", p=128)).then_inc(s_cols, 16)
            for t, source in ((bo_row, bo), (beta_row, ln_beta), (gamma_row, ln_gamma), (bproj_row, b_proj)):
                row(t, source)
            sp.dma_start(w_out["A"][:], w_proj.rearrange("(c p) n -> p c n", p=128)).then_inc(s_w_out["A"], 16)
            for b in range(G):
                sp.sem_inc(s_store[b], 16)

            def next_x(b, group):
                wait_apart(sp, s_norm["A"], (group - 1) * G + b + 1, s_passed_sp)
                wait_apart(sp, s_xbeta, (group - 1) * G + b + 1, s_passed_sp)
                load_x(b, group)

            def store(unit):
                if unit is not None and unit[0] == "B":
                    _, b, group, n = unit
                    wait_apart(sp, s_out_read, n + 1, s_passed_sp)
                    sp.dma_start(out[group * G + b, :, :], y[:, b, :]).then_inc(s_store[b], 16)

            def slot_of(p, slot):
                if p.load and slot == SLOTS - 1:
                    for b in range(G):
                        next_x(b, p.g + 2)
                store(p.before(slot, 2))

            for b in range(G):
                next_x(b, 1)
            each_slot(sp, slot_of)
            for unit in LAST:
                store(unit)
            for b in range(G):
                sp.wait_ge(s_store[b], 16 * (GROUPS + 1))

        @block.gpsimd
        def _(pool):
            nc.gpsimd.memset(ident[:], 0.0).then_inc(s_pool_const, 1)
            nc.gpsimd.memset(eps_col[:], LN_EPS).then_inc(s_pool_const, 1)
            nc.gpsimd.memset(power_col[:], -0.5).then_inc(s_pool_const, 1)
            pool.wait_ge(s_pool_const, 3)
            nc.gpsimd.affine_select(out=ident[:], in_=ident[:], compare_op=ALU.not_equal, fill=1.0, base=0,
                                    pattern=[[-1, 128]], channel_multiplier=1).then_inc(s_pool_const, 1)

            def rstd_of(kind, b, group, n=1):
                pool.wait_ge(s_stats[kind], group * G + b + n)
                nc.gpsimd.tensor_tensor(var_eps[kind][:, b:b + n], mean_var[kind][:, b:b + n, 1],
                                        eps_col[:, 0:n], ALU.add).then_inc(s_vareps[kind], n)
                pool.wait_ge(s_vareps[kind], group * G + b + n)
                nc.gpsimd.tensor_tensor(rstd[kind][:, b:b + n], var_eps[kind][:, b:b + n],
                                        power_col[:, 0:n], ALU.pow).then_inc(s_rstd[kind], n)

            def x_beta_of(b, group):
                pool.wait_ge(s_load[b], (group + 1) * 16)
                if not (isinstance(group, int) and group == 0):
                    pool.wait_ge(s_mid, (group - 1) * G + b + 1)
                nc.gpsimd.tensor_tensor(x_beta[:, b, :], x_in[:, b, :], beta_row[:], ALU.add).then_inc(s_xbeta, 1)

            def x_mid_of(b, group):
                done = (group * G + b) * 2
                pool.wait_ge(s_norm["O"], group * G + b + 1)
                nc.gpsimd.tensor_tensor(attn_ln[:, b, :], attn_ln[:, b, :], gamma_row[:],
                                        ALU.mult).then_inc(s_mid_part, 1)
                pool.wait_ge(s_mid_part, done + 1)
                nc.gpsimd.tensor_tensor(attn_out[:, b, :], attn_out[:, b, :], attn_ln[:, b, :],
                                        ALU.add).then_inc(s_mid_part, 1)
                pool.wait_ge(s_mid_part, done + 2)
                pool.wait_ge(s_xbeta, group * G + b + 1)
                nc.gpsimd.tensor_tensor(x_mid[:, b, :], attn_out[:, b, :], x_beta[:, b, :],
                                        ALU.add).then_inc(s_mid, 1)

            def x_mid_bias_of(b, group):
                pool.wait_ge(s_mid, group * G + b + 1)
                if isinstance(group, int) and group == 0 and b == 0:
                    pool.wait_ge(s_dve_const, DVE_CONSTS)
                if not (isinstance(group, int) and group == 0):
                    pool.wait_ge(s_out_read, unit_of_b(b, group - 1) + 1)
                nc.gpsimd.tensor_tensor(x_mid_bias[:, b, :], x_mid[:, b, :], bo_row[:],
                                        ALU.add).then_inc(s_mid_bias, 1)

            rstd_of("A", 0, 0, n=G)
            pool.wait_ge(s_rows, 16 * 4)
            for b in range(G):
                x_beta_of(b, 0)
            pool.wait_ge(s_cols, 16 * 3)
            nc.gpsimd.tensor_copy(bv_wide[:], bv_col[:].unsqueeze(2).to_broadcast([128, KC, 128])).then_inc(s_pool_const, 1)

            def slot_of(p, slot):
                if p.a and slot in X_MID_SLOTS:
                    rstd_of("O", X_MID_SLOTS.index(slot), p.g)
                if p.ahead and slot < G:
                    rstd_of("A", slot, p.g + 1)
                if p.a and slot >= G:
                    rstd_of("B", slot - G, p.g)
                if p.a and slot in X_MID_SLOTS:
                    x_mid_of(X_MID_SLOTS.index(slot), p.g)
                for b in range(G):
                    if p.ahead and slot == X_BETA_SLOTS[b]:
                        x_beta_of(b, p.g + 1)
                if slot == 7 and p.a:
                    x_mid_bias_of(0, p.g)
                if slot in (0, 1, 2) and p.b:
                    x_mid_bias_of(slot + 1, p.g - 1)

            each_slot(pool, slot_of)

        @block.tensor
        def _(pe):
            def transposed_h(stream, b, group, bank):
                pe.wait_ge(s_norm[stream], group * G + b + 1)
                for c in range(KC):
                    mm = nc.tensor.transpose(bank[:, c * 128:(c + 1) * 128],
                                             normed[stream][:, b, c * 128:(c + 1) * 128], ident[:])
                mm.then_inc(s_T[stream], 1)

            def parts(a_hi, a_lo, b_hi, b_lo):
                return (a_hi, b_hi), (a_hi, b_lo), (a_lo, b_hi)

            def values(stream, b, group, bank):
                pe.wait_ge(s_T_sb[stream], group * G + b + 1)
                for t, (h, w) in enumerate(parts(hT_hi[stream], hT_lo[stream], w_hi[stream], w_lo[stream])):
                    for c in range(KC):
                        mm = nc.tensor.matmul(bank[:, 0:D], h[:, c, b * TOK:(b + 1) * TOK], w[:, c, 2 * D:3 * D],
                                              start=(t == 0 and c == 0), stop=(t == 2 and c == KC - 1))
                mm.then_inc(s_V[stream], 1)

            def queries_keys(stream, m, group, bank):
                pe.wait_ge(s_T_sb[stream], (group + 1) * G)
                for t, (h, w) in enumerate(parts(hT_hi[stream], hT_lo[stream], w_hi[stream], w_lo[stream])):
                    for c in range(KC):
                        mm = nc.tensor.matmul(bank[:], w[:, c, m * 128:(m + 1) * 128], h[:, c, :],
                                              start=(t == 0 and c == 0), stop=(t == 2 and c == KC - 1))
                mm.then_inc(s_QK[stream], 1)

            def qk_copied(p, slot, back=1):
                if slot >= back:
                    if p.piece(slot - back, "QK") is not None:
                        stream, i, group = p.piece(slot - back, "QK")
                        pe.wait_ge(s_QK_sb[stream], group * G + i + 1)
                elif not p.last:
                    pe.wait_ge(s_QK_sb["A"], (p.g + 1) * G)

            def slot_pieces(p, slot, done, kinds):
                for kind, stream, i, group in p.pieces(slot):
                    if kind not in kinds:
                        continue
                    if kind == "V":
                        if not (p.first and slot == 0):
                            pe.wait_ge(s_oT_sb, p.unit(slot) if done is None else done[3])
                        values(stream, i, group, PIECE_BANK["V"])
                    if kind == "T":
                        if p.active(slot):
                            pe.wait_ge(s_negmax, p.unit(slot) * HEADS + KC)
                        elif p.piece(slot - 1, "T") is not None:
                            its_stream, its_i, its_group = p.piece(slot - 1, "T")
                            pe.wait_ge(s_T_sb[its_stream], its_group * G + its_i + 1)
                        transposed_h(stream, i, group, PIECE_BANK["T"])
                    if kind == "QK":
                        if p.active(slot):
                            if done is not None:
                                pe.wait_ge(s_pT_sb[0], done[3] + 1)
                            else:
                                qk_copied(p, slot)
                        elif not p.last:
                            qk_copied(p, slot)
                            pe.wait_ge(s_pT_sb[0], p.unit(slot) if done is None else done[3])
                        elif slot > 1:
                            pe.wait_ge(s_QK_sb[stream], group * G + i - 1)
                        else:
                            pe.wait_ge(s_pT_sb[slot], p.unit(0) + slot - 1)
                            if slot == 0:
                                qk_copied(p, slot)
                        queries_keys(stream, i, group, qk_bank(p, slot))

            def scores(stream, b, group, n, p, slot):
                if b == 0:
                    pe.wait_ge(s_QK_sb[stream], group * G + G - 1)
                if not (p.first and slot == 0):
                    pe.wait_ge(s_negmax, n * HEADS)
                if slot > 0 and p.piece(slot - 1, "T") is not None:
                    its_stream, i, its_group = p.piece(slot - 1, "T")
                    pe.wait_ge(s_T_sb[its_stream], its_group * G + i + 1)
                if slot == 0 and not p.first:
                    pe.wait_ge(s_T_sb["B"], p.g * G)
                tokens = slice(b * TOK, (b + 1) * TOK)
                for h in range(HEADS):
                    c, lanes = h // QUADS, slice(HD * (h % QUADS), HD * (h % QUADS + 1))
                    if b == 0 and h == QUADS:
                        pe.wait_ge(s_QK_sb[stream], group * G + G)
                    nc.tensor.matmul(scores_ps[h], qkT[stream][lanes, c, tokens],
                                     qkT[stream][lanes, KC + c, tokens],
                                     start=True, stop=True).then_inc(s_scores, 1)

            def transposed_probs(n, p, slot):
                first = p is not None and p.first and slot == 1
                for half in range(2):
                    pe.wait_ge(s_exp, n * HEADS + 4 * (half + 1))
                    if not first:
                        pe.wait_ge(s_pT_sb[half], n)
                    if p is not None and half == 0:
                        qk_copied(p, slot, back=1 if p.active(slot) else 0)
                    for i in range(4):
                        mm = nc.tensor.transpose(half_bank[half][:, i * TOK:(i + 1) * TOK],
                                                 probs[(slot - 1) % 2][:, 4 * half + i, :], ident[:])
                    mm.then_inc(s_pT, 1)

            def transposed_recip(n, first=False):
                pe.wait_ge(s_recip_wide, n + 1)
                if first:
                    pe.wait_ge(s_dve_const, DVE_CONSTS)
                else:
                    pe.wait_ge(s_out_read, n)
                for c in range(KC):
                    mm = nc.tensor.transpose(rT_ps[:, c * TOK:(c + 1) * TOK],
                                             recip_wide[:, c * QUADS:(c + 1) * QUADS, :].rearrange("p h d -> p (h d)"),
                                             ident[:])
                mm.then_inc(s_rT, 1)

            def probs_values(stream, b, group, n, p, slot):
                pe.wait_ge(s_V_sb[stream], group * G + b + 1)
                if p is not None and p.piece(slot, "V") is not None:
                    its_stream, i, its_group = p.piece(slot, "V")
                    pe.wait_ge(s_V_sb[its_stream], its_group * G + i + 1)
                for half in range(2):
                    pe.wait_ge(s_pT_sb[half], n + 1)
                    if half == 0 and not (isinstance(n, int) and n == 0):
                        pe.wait_ge(s_oT_sb, n)
                    for i in range(4 * half, 4 * half + 4):
                        h = HEAD_ORDER[i]
                        c, lanes = h // QUADS, slice(HD * (h % QUADS), HD * (h % QUADS + 1))
                        mm = nc.tensor.matmul(oT_ps[lanes, c * TOK:(c + 1) * TOK],
                                              v[stream][:, b, h * HD:(h + 1) * HD],
                                              probsT[:, i, :], start=True, stop=True, skip_group_check=True)
                mm.then_inc(s_pv, 1)

            def output(stream, n):
                pe.wait_ge(s_oT_hi, n + 1)
                for t, (o, w) in enumerate(parts(oT_hi, oT_lo, w_out_hi[stream], w_out_lo[stream])):
                    if o is oT_lo:
                        pe.wait_ge(s_oT_lo, n + 1)
                    for c in range(KC):
                        mm = nc.tensor.matmul(out_ps, o[:, c, :], w[:, c, :],
                                              start=(t == 0 and c == 0), stop=(t == 2 and c == KC - 1))
                mm.then_inc(s_out, 1)

            def value_bias():
                pe.wait_ge(s_pool_const, 5)
                pe.wait_ge(s_w_out["B"], 16)
                for c in range(KC):
                    mm = nc.tensor.matmul(out_ps, bv_wide[:, c, :], w_out["B"][:, c, :],
                                          start=(c == 0), stop=(c == KC - 1))
                mm.then_inc(s_bias_mm, 1)

            def slot_of(p, slot):
                active = p.active(slot)
                if active:
                    stream, b = UNIT_OF_SLOT[slot]
                    scores(stream, b, p.g if stream == "A" else p.g - 1, p.unit(slot), p, slot)
                if p.first and slot == 0:
                    value_bias()
                    for its_stream in "AB":
                        pe.wait_ge(s_w_lo[its_stream], 4)
                second, done = p.before(slot, 2), p.before(slot, 1)
                if not active:
                    slot_pieces(p, slot, done, ("QK",))
                if second is not None:
                    output(second[0], second[3])
                if done is not None:
                    transposed_probs(done[3], p, slot)
                slot_pieces(p, slot, done, ("V",))
                if done is not None:
                    transposed_recip(done[3], p.first and slot == 1)
                if active:
                    slot_pieces(p, slot, done, ("T", "QK"))
                if done is not None:
                    probs_values(*done, p, slot)
                if not active:
                    slot_pieces(p, slot, done, ("T",))

            pe.wait_ge(s_pool_const, 4)
            for kind, stream, i in FIRST_PIECES:
                if kind == "T":
                    transposed_h(stream, i, 0, head_bank[i])
                if kind == "QK":
                    pe.wait_ge(s_w_lo["A"], 2)
                    if i >= 2:
                        pe.wait_ge(s_QK_sb["A"], i - 1)
                    queries_keys(stream, i, 0, half_bank[i % 2])
            each_slot(pe, slot_of)
            output(LAST[0][0], LAST[0][3])
            transposed_probs(LAST[1][3], None, SLOTS)
            transposed_recip(LAST[1][3])
            probs_values(*LAST[1], None, SLOTS)
            output(LAST[1][0], LAST[1][3])

        @block.scalar
        def _(act):
            def copy_piece(kind, stream, i, group, bank):
                if kind == "T":
                    act.wait_ge(s_T[stream], group * G + i + 1)
                    nc.scalar.activation(hT_hi[stream][:, :, i * TOK:(i + 1) * TOK],
                                         bank[:, 0:256].rearrange("p (c t) -> p c t", c=KC),
                                         ACT.Relu).then_inc(s_T_hi[stream], 1)
                if kind == "V":
                    act.wait_ge(s_V[stream], group * G + i + 1)
                    nc.scalar.copy(v[stream][:, i, :], bank[:, 0:D]).then_inc(s_V_sb[stream], 1)
                if kind == "QK":
                    act.wait_ge(s_QK[stream], group * G + i + 1)
                    if stream == "A":
                        nc.scalar.copy(qkT[stream][:, i, :], bank[:]).then_inc(s_QK_sb[stream], 1)
                    else:
                        nc.scalar.activation(qkT[stream][:, i, :], bank[:], ACT.Identity,
                                             bias=bqk_col[:, i:i + 1]).then_inc(s_QK_sb[stream], 1)

            def copy_qk(p, slot):
                for q in p.pieces(slot):
                    if q[0] == "QK":
                        copy_piece(*q, qk_bank(p, slot))

            def round_oT(n):
                act.wait_ge(s_oT_sb, n + 1)
                nc.scalar.copy(oT_hi[:], oT[:]).then_inc(s_oT_hi, 1)

            def probsT_low(n):
                act.wait_ge(s_pT, 2 * n + 1)
                nc.scalar.copy(probsT[:, 0:4, :].rearrange("p h t -> p (h t)"), half_bank[0][:]).then_inc(s_pT_sb[0], 1)

            def recipT_of(n):
                act.wait_ge(s_rT, n + 1)
                nc.scalar.copy(recipT[:].rearrange("p c t -> p (c t)"), rT_ps).then_inc(s_rT_sb, 1)

            def exps(n, slot, heads):
                for i in heads:
                    h = HEAD_ORDER[i]
                    act.wait_ge(s_negmax, n * HEADS + i + 1)
                    nc.scalar.activation(probs[slot % 2][:, i, :], neg_scores[slot % 2][:, i, :], ACT.Exp, scale=-1.0,
                                         bias=neg_max[slot % 2][:, h:h + 1],
                                         accum_out=row_sum[slot % 2][:, h:h + 1]).then_inc(s_exp, 1)

            def slot_of(p, slot):
                second, done = p.before(slot, 2), p.before(slot, 1)
                if second is not None:
                    round_oT(second[3])
                if p.active(slot):
                    exps(p.unit(slot), slot, range(TAIL_AFTER))
                else:
                    copy_qk(p, slot)
                if done is not None:
                    probsT_low(done[3])
                copies_after = COPIES_AFTER if p.piece(slot, "QK") is not None else TAIL_AFTER
                if p.active(slot):
                    exps(p.unit(slot), slot, range(TAIL_AFTER, copies_after))
                for kind in "VT":
                    if kind == "T" and done is not None:
                        recipT_of(done[3])
                    for q in p.pieces(slot):
                        if q[0] == kind:
                            copy_piece(*q, PIECE_BANK[kind])
                if p.active(slot):
                    exps(p.unit(slot), slot, range(copies_after, HEADS - 1))
                    copy_qk(p, slot)
                    exps(p.unit(slot), slot, range(HEADS - 1, HEADS))

            def weights_hi(stream, block):
                if block < 3:
                    cols = slice(block * D, (block + 1) * D)
                    nc.scalar.activation(w_hi[stream][:, :, cols], w_in[stream][:, :, cols], ACT.Copy,
                                         scale=(-SCALE if block == 0 else 1.0)).then_inc(s_w_hi[stream], 1)
                else:
                    nc.scalar.copy(w_out_hi[stream][:], w_out[stream][:]).then_inc(s_w_hi[stream], 1)

            act.wait_ge(s_w_in["A"], 16)
            weights_hi("A", 0)
            weights_hi("A", 1)
            for kind, stream, i in FIRST_PIECES:
                copy_piece(kind, stream, i, 0, {"T": head_bank[i], "QK": half_bank[i % 2]}[kind])
                if kind == "T" and i == G - 1:
                    weights_hi("A", 2)
                    act.wait_ge(s_w_in["B"], 16 * 3)
                    for block in range(3):
                        weights_hi("B", block)
                if kind == "QK" and i < 2:
                    stream = "BA"[i]
                    act.wait_ge(s_w_out[stream], 16)
                    weights_hi(stream, 3)
            each_slot(act, slot_of)
            round_oT(LAST[0][3])
            probsT_low(LAST[1][3])
            recipT_of(LAST[1][3])
            round_oT(LAST[1][3])

        @block.vector
        def _(dve):
            def moments_of(kind, source, b):
                nc.vector.bn_stats(moments[kind][:, b, :], source).then_inc(s_moments[kind], 1)

            def mean_var_of(kind, b, group):
                wait_apart(dve, s_moments[kind], group * G + b + 1, s_passed_dve)
                nc.vector.bn_aggr(mean_var[kind][:, b, :], moments[kind][:, b, :]).then_inc(s_stats[kind], 1)

            def moments_in(b, group):
                dve.wait_ge(s_load[b], (group + 1) * 16)
                moments_of("A", x_in[:, b, :], b)

            def moments_mid(b, group):
                dve.wait_ge(s_mid, group * G + b + 1)
                moments_of("B", x_mid[:, b, :], b)

            def norm(kind, target, source, b, group):
                dve.wait_ge(s_rstd[kind], group * G + b + 1)
                nc.vector.tensor_scalar(target[:, b, :], source[:, b, :], mean_var[kind][:, b, 0:1],
                                        rstd[kind][:, b:b + 1], ALU.subtract, ALU.mult).then_inc(s_norm[kind], 1)

            def recip_of(n, slot):
                dve.wait_ge(s_exp, (n + 1) * HEADS)
                nc.vector.reciprocal(recip[:], row_sum[slot % 2][:]).then_inc(s_recip, 1)

            def widen_recip(n):
                dve.wait_ge(s_recip, n + 1)
                nc.vector.tensor_copy(recip_wide[:],
                                      recip[:].unsqueeze(2).to_broadcast([TOK, HEADS, HD])).then_inc(s_recip_wide, 1)

            def probsT_high(n):
                dve.wait_ge(s_pT, 2 * n + 2)
                nc.vector.tensor_copy(probsT[:, 4:8, :].rearrange("p h t -> p (h t)"),
                                      half_bank[1][:]).then_inc(s_pT_sb[1], 1)

            def mask_max(stream, n, slot, i):
                h = HEAD_ORDER[i]
                if h < QUADS:
                    wait_apart(dve, s_scores, n * HEADS + QUADS + h + 1, s_passed_dve)
                nc.vector.tensor_tensor_reduce(out=neg_scores[slot % 2][:, i, :], in0=scores_ps[h], in1=penalty[stream][:],
                                               scale=1.0, scalar=3e38, op0=ALU.add, op1=ALU.min,
                                               accum_out=neg_max[slot % 2][:, h:h + 1]).then_inc(s_negmax, 1)

            def scale_oT(n):
                dve.wait_ge(s_pv, n + 1)
                dve.wait_ge(s_rT_sb, n + 1)
                nc.vector.tensor_tensor(oT[:].rearrange("p c t -> p (c t)"), oT_ps,
                                        recipT[:].rearrange("p c t -> p (c t)"), ALU.mult).then_inc(s_oT_sb, 1)

            def oT_rest(n):
                dve.wait_ge(s_oT_hi, n + 1)
                nc.vector.tensor_tensor(oT_lo[:], oT[:], oT_hi[:].bitcast(fp32), ALU.subtract).then_inc(s_oT_lo, 1)

            def hT_rest(stream, b, group, bank):
                dve.wait_ge(s_T_hi[stream], group * G + b + 1)
                tokens = slice(b * TOK, (b + 1) * TOK)
                nc.vector.scalar_tensor_tensor(
                    out=hT_lo[stream][:, :, tokens], in0=bank[:, 0:256].rearrange("p (c t) -> p c t", c=KC),
                    scalar=0.0, in1=hT_hi[stream][:, :, tokens].bitcast(fp32),
                    op0=ALU.max, op1=ALU.subtract).then_inc(s_T_sb[stream], 1)

            def read_output(done):
                stream, b, group, n = done
                dve.wait_ge(s_out, n + 1)
                if stream == "A":
                    nc.vector.tensor_tensor(attn_out[:, b, :], out_ps, bproj_row[:], ALU.add).then_inc(s_out_read, 1)
                else:
                    dve.wait_ge(s_mid_bias, group * G + b + 1)
                    dve.wait_ge(s_store[b], 16 * (group + 1))
                    nc.vector.tensor_tensor(y[:, b, :], out_ps, x_mid_bias[:, b, :], ALU.add).then_inc(s_out_read, 1)

            def slot_of(p, slot):
                second, done, n = p.before(slot, 2), p.before(slot, 1), p.unit(slot)
                norm_a, norm_b = p.ahead and slot < G, p.a and slot >= G
                if second is not None:
                    scale_oT(second[3])
                if p.first and slot in X_MID_SLOTS:
                    norm("O", attn_ln, attn_out, X_MID_SLOTS.index(slot), p.g)
                if norm_a:
                    moments_in(slot, p.g + 1)
                    mean_var_of("A", slot, p.g + 1)
                if norm_b:
                    moments_mid(slot - G, p.g)
                    mean_var_of("B", slot - G, p.g)
                if second is not None:
                    oT_rest(second[3])
                for head in range(HEADS):
                    if p.active(slot):
                        mask_max(UNIT_OF_SLOT[slot][0], n, slot, head)
                    if head == RECIP_AFTER - 1 and done is not None:
                        recip_of(done[3], slot - 1)
                    if head == WIDEN_AFTER - 1 and done is not None:
                        widen_recip(done[3])
                    if head == OUT_AFTER - 1 and second is not None:
                        read_output(second)
                    if head == NORM_AFTER - 1 and norm_a:
                        norm("A", normed["A"], x_in, slot, p.g + 1)
                    if head == NORM_AFTER - 1 and norm_b:
                        norm("B", normed["B"], x_mid, slot - G, p.g)
                if p.a and not p.first and slot in X_MID_SLOTS:
                    norm("O", attn_ln, attn_out, X_MID_SLOTS.index(slot), p.g)
                if done is not None:
                    probsT_high(done[3])
                if second is not None and second[0] == "A":
                    dve.wait_ge(s_out_read, second[3] + 1)
                    moments_of("O", attn_out[:, second[1], :], second[1])
                    mean_var_of("O", second[1], p.g)
                for q in p.pieces(slot):
                    if q[0] == "T":
                        hT_rest(*q[1:], PIECE_BANK["T"])

                if p.first and slot == 0:
                    dve.wait_ge(s_rows, 16 * 4)
                    dve.wait_ge(s_bias_mm, 1)
                    nc.vector.tensor_tensor(bo_row[:], out_ps, bo_row[:], ALU.add).then_inc(s_dve_const, 1)

            def weights_lo(stream, block):
                dve.wait_ge(s_w_hi[stream], block + 1)
                if block < 3:
                    cols = slice(block * D, (block + 1) * D)
                    nc.vector.scalar_tensor_tensor(out=w_lo[stream][:, :, cols], in0=w_in[stream][:, :, cols],
                                                   scalar=(-SCALE if block == 0 else 1.0),
                                                   in1=w_hi[stream][:, :, cols].bitcast(fp32),
                                                   op0=ALU.mult, op1=ALU.subtract).then_inc(s_w_lo[stream], 1)
                else:
                    nc.vector.tensor_tensor(w_out_lo[stream][:], w_out[stream][:], w_out_hi[stream][:].bitcast(fp32),
                                            ALU.subtract).then_inc(s_w_lo[stream], 1)

            for b in range(G):
                moments_in(b, 0)
            for b in range(G):
                mean_var_of("A", b, 0)
            for b in range(G):
                norm("A", normed["A"], x_in, b, 0)
            weights_lo("A", 0)
            weights_lo("A", 1)
            for kind, stream, i in FIRST_PIECES:
                if kind == "T":
                    hT_rest(stream, i, 0, head_bank[i])
            weights_lo("A", 2)
            for block in range(3):
                weights_lo("B", block)
            dve.wait_ge(s_adj, 16)
            dve.wait_ge(s_cols, 16 * 3)
            nc.vector.tensor_scalar(penalty["A"][:], adjacency[:], 0.0, MASKED_FIRST,
                                    ALU.is_equal, ALU.mult).then_inc(s_dve_const, 1)
            nc.vector.tensor_scalar(penalty["B"][:], adjacency[:], 1.0, -MASKED_SECOND,
                                    ALU.subtract, ALU.mult).then_inc(s_dve_const, 1)
            nc.vector.tensor_scalar(bqk_col[:, 0:KC], bqk_col[:, 0:KC], -SCALE, None, ALU.mult).then_inc(s_dve_const, 1)
            for stream in "BA":
                weights_lo(stream, 3)
            dve.wait_ge(s_dve_const, DVE_CONSTS - 1)
            each_slot(dve, slot_of)
            for last in LAST:
                scale_oT(last[3])
                oT_rest(last[3])
                if last is LAST[0]:
                    recip_of(LAST[1][3], SLOTS - 1)
                    widen_recip(LAST[1][3])
                    read_output(last)
                    probsT_high(LAST[1][3])
            read_output(LAST[1])


_INS = ["x", "adj", "L0_gnn_w_qkv", "L0_gnn_w_proj", "L0_gnn_b_proj", "L0_gnn_ln_gamma", "L0_gnn_ln_beta",
        "L1_gnn_Wq", "L1_gnn_bq", "L1_gnn_Wk", "L1_gnn_bk", "L1_gnn_Wv", "L1_gnn_bv", "L1_gnn_Wo", "L1_gnn_bo"]


def kernel(**inputs):
    import numpy as np
    import concourse.bacc as bacc
    from concourse.bass_utils import run_bass_kernel_spmd

    nc = bacc.Bacc("TRN2", target_bir_lowering=False, num_devices=1)
    arrays, args = {}, []
    for name in _INS:
        a = np.ascontiguousarray(inputs[name])
        arrays[f"in_{name}"] = a
        args.append(nc.dram_tensor(f"in_{name}", a.shape, mybir.dt.from_np(a.dtype), kind="ExternalInput").ap())
    args.append(nc.dram_tensor("out_x", (BATCHES, TOK, D), fp32, kind="ExternalOutput").ap())
    gnn_stack_kernel(nc, *args)
    return run_bass_kernel_spmd(nc, [arrays], core_ids=[0]).results[0]["out_x"]
```
